# Optimizing a Trainium2 kernel written in Bass

```python
import numpy as np
import jax
import jax.numpy as jnp

def _softmax(x, axis=-1):
    return jax.nn.softmax(x, axis=axis)

def _gelu(x):
    return jax.nn.gelu(x, approximate=True)

def _silu(x):
    return jax.nn.silu(x)

def _sigmoid(x):
    return jax.nn.sigmoid(x)

def _layernorm(x, axis=-1, eps=1e-05):
    m = jnp.mean(x, axis=axis, keepdims=True)
    v = jnp.var(x, axis=axis, keepdims=True)
    return (x - m) / jnp.sqrt(v + eps)

def _scatter_add(tgt, idx, src, axis=0):
    return tgt.at[idx].add(src)

def _segment_sum(src, seg, n):
    return jax.ops.segment_sum(src, seg, n)
kernel_name = 'mk_decoder_postln_d1_seqx_r4_7fdec7'

def setup_inputs(seed: int=0):
    np.random.seed(seed)
    _w = jnp.asarray

    def _rec_inputs():
        import jax
        import jax.numpy as jnp
        _rk = jax.random.key(seed)
        x = 7.22e-05 + 1 * jax.random.normal(jax.random.fold_in(_rk, 1), (8, 256, 256), jnp.float32)
        _lenS = 256 - jax.random.randint(jax.random.fold_in(_rk, 7), (8,), 0, max(1, 256 // 4) + 1, jnp.int32)
        _lenS2 = 77 - jax.random.randint(jax.random.fold_in(_rk, 8), (8,), 0, max(1, 77 // 4) + 1, jnp.int32)
        _ctx_1024P = jax.random.normal(jax.random.fold_in(_rk, 11), (8, 16, 256), jnp.float32)
        _ctx_1024c = jax.random.dirichlet(jax.random.fold_in(_rk, 511), 0.3 * jnp.ones((16,), jnp.float32), (8, 77))
        _ctx_1024t = jnp.einsum('bsk,bkd->bsd', _ctx_1024c, _ctx_1024P)
        _ctx_1024t = _ctx_1024t * jax.lax.rsqrt(jnp.mean(jnp.square(_ctx_1024t)) + 1e-12) * 0.953939
        ctx_1024 = -1.39393e-06 + 0.999914 * (_ctx_1024t + 0.3 * jax.random.normal(jax.random.fold_in(_rk, 611), (8, 77, 256), jnp.float32))
        return (x, ctx_1024)
    x, ctx_1024 = _rec_inputs()

    def _L0_attn_setup():
        import jax, jax.numpy as jnp
        import numpy as np
        import math
        EPS = 1e-06

        def favorplus_features(x, proj):
            xw = jnp.einsum('bhtd,hmd->bhtm', x, proj)
            xw = xw - jnp.max(xw, axis=-1, keepdims=True)
            x_norm_sq = jnp.sum(x * x, axis=-1, keepdims=True)
            return jnp.exp(xw) * jnp.exp(-0.5 * x_norm_sq) + EPS
        key = jax.random.key(seed)
        ks = jax.random.split(key, 6)
        B, T, d = (2, 1024, 256)
        h, m = (16, 64)
        dk = d // h
        s = 1.0 / math.sqrt(d)
        return {'x': jax.random.normal(ks[0], (B, T, d), dtype=jnp.float32), 'Wq': jax.random.normal(ks[1], (d, d), dtype=jnp.float32) * s, 'Wk': jax.random.normal(ks[2], (d, d), dtype=jnp.float32) * s, 'Wv': jax.random.normal(ks[3], (d, d), dtype=jnp.float32) * s, 'Wo': jax.random.normal(ks[4], (d, d), dtype=jnp.float32) * s, 'bo': jnp.zeros((d,), dtype=jnp.float32), 'proj': jax.random.normal(ks[5], (h, m, dk), dtype=jnp.float32)}
    _L0_attn_all = _L0_attn_setup()
    _L0_attn_in = {k: v for k, v in _L0_attn_all.items() if k in ('Wq', 'Wk', 'Wv', 'Wo', 'bo', 'proj')}
    del _L0_attn_all

    def _L0_xattn_setup():
        import jax, jax.numpy as jnp
        import numpy as np
        DIM = 256
        N_HEADS = 16
        HEAD_DIM = DIM // N_HEADS
        GAMMA = 10.0

        def larope_cos_sin(seq_len, gamma, head_dim):
            inv_freq = 1.0 / 10000.0 ** (jnp.arange(0, head_dim, 2, dtype=jnp.float32) / head_dim)
            t = jnp.arange(seq_len, dtype=jnp.float32)
            freqs = jnp.outer(gamma * (t / seq_len), inv_freq)
            emb = jnp.concatenate([freqs, freqs], axis=-1)
            return (jnp.cos(emb), jnp.sin(emb))

        def apply_rope(x, cos, sin):
            d = x.shape[-1] // 2
            x1, x2 = (x[..., :d], x[..., d:])
            c = cos[None, None, :, :d]
            s = sin[None, None, :, :d]
            return jnp.concatenate([x1 * c - x2 * s, x1 * s + x2 * c], axis=-1)
        key = jax.random.key(seed)
        ks = jax.random.split(key, 11)
        B, Lq, Lk = (4, 512, 256)
        std = 1.0 / np.sqrt(DIM)
        inp = {'query': jax.random.normal(ks[0], (B, Lq, DIM), dtype=jnp.float32), 'key': jax.random.normal(ks[1], (B, Lk, DIM), dtype=jnp.float32), 'value': jax.random.normal(ks[2], (B, Lk, DIM), dtype=jnp.float32), 'Wq': jax.random.normal(ks[3], (DIM, DIM), dtype=jnp.float32) * std, 'bq': jnp.zeros((DIM,), dtype=jnp.float32), 'Wk': jax.random.normal(ks[4], (DIM, DIM), dtype=jnp.float32) * std, 'bk': jnp.zeros((DIM,), dtype=jnp.float32), 'Wv': jax.random.normal(ks[5], (DIM, DIM), dtype=jnp.float32) * std, 'bv': jnp.zeros((DIM,), dtype=jnp.float32), 'Wo': jax.random.normal(ks[6], (DIM, DIM), dtype=jnp.float32) * std, 'bo': jnp.zeros((DIM,), dtype=jnp.float32)}
        return inp
    _L0_xattn_all = _L0_xattn_setup()
    _L0_xattn_in = {k: v for k, v in _L0_xattn_all.items() if k in ('Wq', 'bq', 'Wk', 'bk', 'Wv', 'bv', 'Wo', 'bo')}
    del _L0_xattn_all

    def _L0_ffn_setup():
        import jax, jax.numpy as jnp
        import numpy as np
        EPS = 1e-05

        def _ln(x, g, b):
            mu = jnp.mean(x, axis=-1, keepdims=True)
            var = jnp.mean(jnp.square(x - mu), axis=-1, keepdims=True)
            return (x - mu) * jax.lax.rsqrt(var + EPS) * g + b

        def _forward(x, index_b, index_t, sw1, sb1, sw2, sb2, sw3, sb3, s_ln_g, s_ln_b, sg_w, sg_b, eg_w, eg_b, exp_bias, ew1, eb1, ew2, eb2, ew3, eb3, sel_ln_g, sel_ln_b):
            x1 = jnp.einsum('btd,hd->bth', x, sw1) + sb1
            x2 = jnp.einsum('btd,hd->bth', x, sw2) + sb2
            sh = _ln(jax.nn.silu(x1) * x2, s_ln_g, s_ln_b)
            shared_out = jnp.einsum('bth,dh->btd', sh, sw3) + sb3
            x_moe = x[index_b, index_t]
            shared_scores = jax.nn.sigmoid(x_moe @ sg_w.T + sg_b)
            expert_scores = jax.nn.sigmoid(x_moe @ eg_w.T + eg_b)
            top1_idx = jnp.argmax(expert_scores + exp_bias, axis=-1)
            top1_score = jnp.take_along_axis(expert_scores, top1_idx[:, None], axis=-1)
            weights = jax.nn.softmax(jnp.concatenate([shared_scores, top1_score], axis=-1), axis=-1)
            shared_w, expert_w = (weights[:, 0], weights[:, 1])
            shared_moe_out = shared_out[index_b, index_t] * shared_w[:, None]
            h1 = jnp.einsum('md,ehd->meh', x_moe, ew1) + eb1
            h2 = jnp.einsum('md,ehd->meh', x_moe, ew2) + eb2
            z = _ln(jax.nn.silu(h1) * h2, sel_ln_g, sel_ln_b)
            out_all = jnp.einsum('meh,edh->med', z, ew3) + eb3
            expert_out = jnp.take_along_axis(out_all, top1_idx[:, None, None], axis=1)[:, 0]
            expert_moe_out = expert_out * expert_w[:, None]
            final_out = shared_out.at[index_b, index_t].set(shared_moe_out + expert_moe_out)
            return final_out
        B, T, D, E, H, M = (2, 512, 256, 8, 128, 512)
        key = jax.random.key(seed)
        ks = jax.random.split(key, 24)
        s = 0.02
        inp = {}
        inp['x'] = jax.random.normal(ks[0], (B, T, D), jnp.float32)
        flat = jnp.arange(M, dtype=jnp.int32) * 2
        inp['index_b'] = flat // T
        inp['index_t'] = flat % T
        inp['sw1'] = jax.random.normal(ks[1], (H, D), jnp.float32) * s
        inp['sb1'] = jnp.zeros((H,), jnp.float32)
        inp['sw2'] = jax.random.normal(ks[2], (H, D), jnp.float32) * s
        inp['sb2'] = jnp.zeros((H,), jnp.float32)
        inp['sw3'] = jax.random.normal(ks[3], (D, H), jnp.float32) * s
        inp['sb3'] = jnp.zeros((D,), jnp.float32)
        inp['s_ln_g'] = jnp.ones((H,), jnp.float32)
        inp['s_ln_b'] = jnp.zeros((H,), jnp.float32)
        inp['sg_w'] = jax.random.normal(ks[4], (1, D), jnp.float32) * s
        inp['sg_b'] = jnp.zeros((1,), jnp.float32)
        inp['eg_w'] = jax.random.normal(ks[5], (E, D), jnp.float32) * s
        inp['eg_b'] = jnp.zeros((E,), jnp.float32)
        inp['exp_bias'] = jnp.zeros((E,), jnp.float32)
        inp['ew1'] = jax.random.normal(ks[6], (E, H, D), jnp.float32) * s
        inp['eb1'] = jnp.zeros((E, H), jnp.float32)
        inp['ew2'] = jax.random.normal(ks[7], (E, H, D), jnp.float32) * s
        inp['eb2'] = jnp.zeros((E, H), jnp.float32)
        inp['ew3'] = jax.random.normal(ks[8], (E, D, H), jnp.float32) * s
        inp['eb3'] = jnp.zeros((E, D), jnp.float32)
        inp['sel_ln_g'] = jnp.ones((H,), jnp.float32)
        inp['sel_ln_b'] = jnp.zeros((H,), jnp.float32)
        return inp
    _L0_ffn_all = _L0_ffn_setup()
    _L0_ffn_in = {k: v for k, v in _L0_ffn_all.items() if k in ('index_b', 'index_t', 'sw1', 'sb1', 'sw2', 'sb2', 'sw3', 'sb3', 's_ln_g', 's_ln_b', 'sg_w', 'sg_b', 'eg_w', 'eg_b', 'exp_bias', 'ew1', 'eb1', 'ew2', 'eb2', 'ew3', 'eb3', 'sel_ln_g', 'sel_ln_b')}
    del _L0_ffn_all
    return {'x': x, 'ctx_1024': ctx_1024, 'L0_attn_Wq': _L0_attn_in['Wq'], 'L0_attn_Wk': _L0_attn_in['Wk'], 'L0_attn_Wv': _L0_attn_in['Wv'], 'L0_attn_Wo': _L0_attn_in['Wo'], 'L0_attn_bo': _L0_attn_in['bo'], 'L0_attn_proj': _L0_attn_in['proj'], 'L0_xattn_Wq': _L0_xattn_in['Wq'], 'L0_xattn_bq': _L0_xattn_in['bq'], 'L0_xattn_Wk': _L0_xattn_in['Wk'], 'L0_xattn_bk': _L0_xattn_in['bk'], 'L0_xattn_Wv': _L0_xattn_in['Wv'], 'L0_xattn_bv': _L0_xattn_in['bv'], 'L0_xattn_Wo': _L0_xattn_in['Wo'], 'L0_xattn_bo': _L0_xattn_in['bo'], 'L0_ffn_index_b': _L0_ffn_in['index_b'], 'L0_ffn_index_t': _L0_ffn_in['index_t'], 'L0_ffn_sw1': _L0_ffn_in['sw1'], 'L0_ffn_sb1': _L0_ffn_in['sb1'], 'L0_ffn_sw2': _L0_ffn_in['sw2'], 'L0_ffn_sb2': _L0_ffn_in['sb2'], 'L0_ffn_sw3': _L0_ffn_in['sw3'], 'L0_ffn_sb3': _L0_ffn_in['sb3'], 'L0_ffn_s_ln_g': _L0_ffn_in['s_ln_g'], 'L0_ffn_s_ln_b': _L0_ffn_in['s_ln_b'], 'L0_ffn_sg_w': _L0_ffn_in['sg_w'], 'L0_ffn_sg_b': _L0_ffn_in['sg_b'], 'L0_ffn_eg_w': _L0_ffn_in['eg_w'], 'L0_ffn_eg_b': _L0_ffn_in['eg_b'], 'L0_ffn_exp_bias': _L0_ffn_in['exp_bias'], 'L0_ffn_ew1': _L0_ffn_in['ew1'], 'L0_ffn_eb1': _L0_ffn_in['eb1'], 'L0_ffn_ew2': _L0_ffn_in['ew2'], 'L0_ffn_eb2': _L0_ffn_in['eb2'], 'L0_ffn_ew3': _L0_ffn_in['ew3'], 'L0_ffn_eb3': _L0_ffn_in['eb3'], 'L0_ffn_sel_ln_g': _L0_ffn_in['sel_ln_g'], 'L0_ffn_sel_ln_b': _L0_ffn_in['sel_ln_b']}

def reference(x, ctx_1024, L0_attn_Wq, L0_attn_Wk, L0_attn_Wv, L0_attn_Wo, L0_attn_bo, L0_attn_proj, L0_xattn_Wq, L0_xattn_bq, L0_xattn_Wk, L0_xattn_bk, L0_xattn_Wv, L0_xattn_bv, L0_xattn_Wo, L0_xattn_bo, L0_ffn_index_b, L0_ffn_index_t, L0_ffn_sw1, L0_ffn_sb1, L0_ffn_sw2, L0_ffn_sb2, L0_ffn_sw3, L0_ffn_sb3, L0_ffn_s_ln_g, L0_ffn_s_ln_b, L0_ffn_sg_w, L0_ffn_sg_b, L0_ffn_eg_w, L0_ffn_eg_b, L0_ffn_exp_bias, L0_ffn_ew1, L0_ffn_eb1, L0_ffn_ew2, L0_ffn_eb2, L0_ffn_ew3, L0_ffn_eb3, L0_ffn_sel_ln_g, L0_ffn_sel_ln_b):
    import jax
    import jax.numpy as jnp

    def _L0_attn_ref(x, Wq, Wk, Wv, Wo, bo, proj):
        import jax, jax.numpy as jnp
        import numpy as np
        import math
        EPS = 1e-06

        def favorplus_features(x, proj):
            xw = jnp.einsum('bhtd,hmd->bhtm', x, proj)
            xw = xw - jnp.max(xw, axis=-1, keepdims=True)
            x_norm_sq = jnp.sum(x * x, axis=-1, keepdims=True)
            return jnp.exp(xw) * jnp.exp(-0.5 * x_norm_sq) + EPS
        B, T, d = x.shape
        h, m, dk = proj.shape

        def heads(W):
            y = jnp.einsum('btd,ed->bte', x, W)
            return y.reshape(B, T, h, dk).transpose(0, 2, 1, 3)
        Q = heads(Wq) / math.sqrt(dk)
        K = heads(Wk) / math.sqrt(dk)
        V = heads(Wv)
        inv_sqrt_m = 1.0 / math.sqrt(m)
        phiQ = favorplus_features(Q, proj) * inv_sqrt_m
        phiK = favorplus_features(K, proj) * inv_sqrt_m
        KV = jnp.einsum('bhtm,bhtd->bhmd', phiK, V)
        Ksum = jnp.sum(phiK, axis=2)
        num = jnp.einsum('bhtm,bhmd->bhtd', phiQ, KV)
        den = jnp.einsum('bhtm,bhm->bht', phiQ, Ksum)[..., None] + EPS
        out_heads = num / den
        merged = out_heads.transpose(0, 2, 1, 3).reshape(B, T, d)
        return jnp.einsum('btd,ed->bte', merged, Wo) + bo

    def _L0_xattn_ref(query, key, value, Wq, bq, Wk, bk, Wv, bv, Wo, bo):
        import jax, jax.numpy as jnp
        import numpy as np
        DIM = 256
        N_HEADS = 16
        HEAD_DIM = DIM // N_HEADS
        GAMMA = 10.0

        def larope_cos_sin(seq_len, gamma, head_dim):
            inv_freq = 1.0 / 10000.0 ** (jnp.arange(0, head_dim, 2, dtype=jnp.float32) / head_dim)
            t = jnp.arange(seq_len, dtype=jnp.float32)
            freqs = jnp.outer(gamma * (t / seq_len), inv_freq)
            emb = jnp.concatenate([freqs, freqs], axis=-1)
            return (jnp.cos(emb), jnp.sin(emb))

        def apply_rope(x, cos, sin):
            d = x.shape[-1] // 2
            x1, x2 = (x[..., :d], x[..., d:])
            c = cos[None, None, :, :d]
            s = sin[None, None, :, :d]
            return jnp.concatenate([x1 * c - x2 * s, x1 * s + x2 * c], axis=-1)
        B, Lq, _ = query.shape
        Lk = key.shape[1]
        scale = HEAD_DIM ** (-0.5)

        def proj(x, W, b, L):
            y = x @ W.T + b
            return y.reshape(B, L, N_HEADS, HEAD_DIM).transpose(0, 2, 1, 3)
        q = proj(query, Wq, bq, Lq)
        k = proj(key, Wk, bk, Lk)
        v = proj(value, Wv, bv, Lk)
        q_cos, q_sin = larope_cos_sin(Lq, GAMMA, HEAD_DIM)
        k_cos, k_sin = larope_cos_sin(Lk, GAMMA, HEAD_DIM)
        q = apply_rope(q, q_cos, q_sin)
        k = apply_rope(k, k_cos, k_sin)
        scores = jnp.einsum('bhqd,bhkd->bhqk', q, k) * scale
        attn = jax.nn.softmax(scores, axis=-1)
        out = jnp.einsum('bhqk,bhkd->bhqd', attn, v)
        out = out.transpose(0, 2, 1, 3).reshape(B, Lq, DIM)
        return out @ Wo.T + bo

    def _L0_ffn_ref(x, index_b, index_t, sw1, sb1, sw2, sb2, sw3, sb3, s_ln_g, s_ln_b, sg_w, sg_b, eg_w, eg_b, exp_bias, ew1, eb1, ew2, eb2, ew3, eb3, sel_ln_g, sel_ln_b):
        import jax, jax.numpy as jnp
        import numpy as np
        EPS = 1e-05

        def _ln(x, g, b):
            mu = jnp.mean(x, axis=-1, keepdims=True)
            var = jnp.mean(jnp.square(x - mu), axis=-1, keepdims=True)
            return (x - mu) * jax.lax.rsqrt(var + EPS) * g + b

        def _forward(x, index_b, index_t, sw1, sb1, sw2, sb2, sw3, sb3, s_ln_g, s_ln_b, sg_w, sg_b, eg_w, eg_b, exp_bias, ew1, eb1, ew2, eb2, ew3, eb3, sel_ln_g, sel_ln_b):
            x1 = jnp.einsum('btd,hd->bth', x, sw1) + sb1
            x2 = jnp.einsum('btd,hd->bth', x, sw2) + sb2
            sh = _ln(jax.nn.silu(x1) * x2, s_ln_g, s_ln_b)
            shared_out = jnp.einsum('bth,dh->btd', sh, sw3) + sb3
            x_moe = x[index_b, index_t]
            shared_scores = jax.nn.sigmoid(x_moe @ sg_w.T + sg_b)
            expert_scores = jax.nn.sigmoid(x_moe @ eg_w.T + eg_b)
            top1_idx = jnp.argmax(expert_scores + exp_bias, axis=-1)
            top1_score = jnp.take_along_axis(expert_scores, top1_idx[:, None], axis=-1)
            weights = jax.nn.softmax(jnp.concatenate([shared_scores, top1_score], axis=-1), axis=-1)
            shared_w, expert_w = (weights[:, 0], weights[:, 1])
            shared_moe_out = shared_out[index_b, index_t] * shared_w[:, None]
            h1 = jnp.einsum('md,ehd->meh', x_moe, ew1) + eb1
            h2 = jnp.einsum('md,ehd->meh', x_moe, ew2) + eb2
            z = _ln(jax.nn.silu(h1) * h2, sel_ln_g, sel_ln_b)
            out_all = jnp.einsum('meh,edh->med', z, ew3) + eb3
            expert_out = jnp.take_along_axis(out_all, top1_idx[:, None, None], axis=1)[:, 0]
            expert_moe_out = expert_out * expert_w[:, None]
            final_out = shared_out.at[index_b, index_t].set(shared_moe_out + expert_moe_out)
            return final_out
        return _forward(x, index_b, index_t, sw1, sb1, sw2, sb2, sw3, sb3, s_ln_g, s_ln_b, sg_w, sg_b, eg_w, eg_b, exp_bias, ew1, eb1, ew2, eb2, ew3, eb3, sel_ln_g, sel_ln_b)
    x = _layernorm(x + _L0_attn_ref(x, L0_attn_Wq, L0_attn_Wk, L0_attn_Wv, L0_attn_Wo, L0_attn_bo, L0_attn_proj), axis=-1)
    x = _layernorm(x + _L0_xattn_ref(x, ctx_1024, ctx_1024, L0_xattn_Wq, L0_xattn_bq, L0_xattn_Wk, L0_xattn_bk, L0_xattn_Wv, L0_xattn_bv, L0_xattn_Wo, L0_xattn_bo), axis=-1)
    x = _layernorm(x + _L0_ffn_ref(x, L0_ffn_index_b, L0_ffn_index_t, L0_ffn_sw1, L0_ffn_sb1, L0_ffn_sw2, L0_ffn_sb2, L0_ffn_sw3, L0_ffn_sb3, L0_ffn_s_ln_g, L0_ffn_s_ln_b, L0_ffn_sg_w, L0_ffn_sg_b, L0_ffn_eg_w, L0_ffn_eg_b, L0_ffn_exp_bias, L0_ffn_ew1, L0_ffn_eb1, L0_ffn_ew2, L0_ffn_eb2, L0_ffn_ew3, L0_ffn_eb3, L0_ffn_sel_ln_g, L0_ffn_sel_ln_b), axis=-1)
    return x

_drawn_inputs = setup_inputs


def setup_inputs(seed=0):
    import zlib

    import numpy as np

    out = dict(_drawn_inputs(seed))
    spreads = {'L0_attn_bo': (0.0, 0.1),
     'L0_xattn_bq': (0.0, 0.385),
     'L0_xattn_bk': (0.0, 0.8),
     'L0_xattn_bv': (0.0, 0.1),
     'L0_xattn_bo': (0.0, 0.1),
     'L0_ffn_sb1': (0.0, 0.1),
     'L0_ffn_sb2': (0.0, 0.1),
     'L0_ffn_sb3': (0.0, 0.1),
     'L0_ffn_s_ln_g': (1.0, 0.2),
     'L0_ffn_s_ln_b': (0.0, 0.363),
     'L0_ffn_eg_b': (0.0, 0.666),
     'L0_ffn_exp_bias': (0.0, 0.1),
     'L0_ffn_eb1': (0.0, 0.541),
     'L0_ffn_eb2': (0.0, 0.597),
     'L0_ffn_eb3': (0.0, 0.458),
     'L0_ffn_sel_ln_g': (1.0, 0.6),
     'L0_ffn_sel_ln_b': (0.0, 0.8)}
    factors = {'L0_attn_Wq': 2.921, 'L0_attn_proj': 2.754, 'L0_ffn_sg_w': 24.095}
    for name, (base, spread) in spreads.items():
        noise = np.random.default_rng([zlib.crc32(name.encode()), seed]).standard_normal(out[name].shape)
        drawn = base * np.exp(spread * noise) if base else spread * noise
        out[name] = jnp.asarray(drawn.astype(out[name].dtype))
    for name, factor in factors.items():
        out[name] = (out[name] * factor).astype(out[name].dtype)
    return out
```

```python
from contextlib import ExitStack

import numpy as np

import concourse.bass as bass
from concourse import mybir

ALU = mybir.AluOpType
ACT = mybir.ActivationFunctionType
F32 = mybir.dt.float32
I32 = mybir.dt.int32
U32 = mybir.dt.uint32
AX_X = mybir.AxisListType.X

P = 128
B, T, D = 8, 256, 256
TT = T // P
DC = D // P
H, M, DK = 16, 64, 16
DV = DK + 1
HC = H // DC
PAIRS = H // 2
LK = 77
CT = B * LK
NE, FH, NM = 8, 128, 512
NU = 1 + NE
MT = NM // P
EPS_PHI = 1e-6
EPS_LN = 1e-5
SCALE = DK ** -0.5
FAR = 4096.0

C_ID, C_CTR, C_COSQ, C_SINQ = 0, 128, 256, 256 + TT * D
C_COST = C_SINQ + TT * D
C_SINT = C_COST + T
C_COSK = C_SINT + T
C_SINK = C_COSK + LK
C_MASK = C_SINK + LK
C_HALF = C_MASK + 4
C_REV = C_HALF + HC
C_END = C_REV + NE


def after(eng, sem, per, b, k):
    if isinstance(b, int) and b < 0:
        return
    eng.wait_ge(sem, b * per + k)


def after_plainly(eng, zeroed, *events):
    targets = [(s, b * per + k if isinstance(b, int) else eng.compute_val(b * per + k)) for s, per, b, k in events
               if not (isinstance(b, int) and b < 0)]
    eng.wait_ge(zeroed, 5)
    for s, value in targets:
        eng.wait_ge(s, value)


def decoder_layer(nc, g, out):
    ctx = ExitStack()
    with ctx:
        def sb(name, shape, dt=F32):
            return ctx.enter_context(nc.sbuf_tensor(name, shape, dt))

        def pb(name, cols):
            return ctx.enter_context(nc.psum_tensor(name, [P, cols], F32))

        def sem(name):
            return ctx.enter_context(nc.semaphore(name))

        x2_dram = nc.dram_tensor("x2_rows", [B * T, D], F32, kind="Internal").ap()

        PX = pb("psum_features", 1024)
        PA = pb("psum_a", 512)
        PS = pb("psum_scores", 1024)
        PT = pb("psum_probs_t", 512)
        PB = pb("psum_b", 512)
        PC = pb("psum_c", 512)

        cst = sb("cst", [P, C_END])
        ident = cst[:, C_ID:C_ID + P]
        center = cst[:, C_CTR:C_CTR + P]
        cosq = cst[:, C_COSQ:C_COSQ + TT * D]
        sinq = cst[:, C_SINQ:C_SINQ + TT * D]
        cosT = cst[:, C_COST:C_COST + T]
        sinT = cst[:, C_SINT:C_SINT + T]
        cosk = cst[:, C_COSK:C_COSK + LK]
        sink = cst[:, C_SINK:C_SINK + LK]
        head_mask = cst[:, C_MASK:C_MASK + 4]
        half_blocks = cst[:, C_HALF:C_HALF + HC]
        rev_index = cst[:, C_REV:C_REV + NE]
        names = ("aq", "ak", "av", "ao", "xk", "xkr", "xv", "xq", "xo", "s12")
        weights = sb("weights", [P, len(names), DC, D])
        w = {n: weights[:, j] for j, n in enumerate(names)}
        w3s = sb("w3s", [P, D])
        projbd = sb("projbd", [P, DC, HC * M])
        ctxT = sb("ctxT", [P, DC, CT])
        cols = sb("cols", [P, 14])
        BQ, BQR, BK, BKR, BV, SB1, SB2, SG, SLB = 0, 2, 4, 6, 8, 10, 11, 12, 13
        rows = sb("rows", [1, 3, D])
        bo_a = sb("bo_a", [P, D])
        bo_b = sb("bo_b", [P, D])
        c3_s = sb("c3_s", [P, D])
        w3c_s = sb("w3c_s", [P, D])
        w3g = sb("w3g", [P, D])
        ones = sb("ones", [P, P])
        minus_half = sb("minus_half", [P, MT])
        rbqT = sb("rbqT", [P, DC, T])
        ktr = sb("ktr", [P, DC, CT])
        ktt = sb("ktt", [P, 2, 2, CT // 2])
        vx = sb("vx", [LK, B, H, DV])
        rq_tmp = sb("rq_tmp", [P, DC, T])

        xT = sb("xT", [P, DC, T])
        xrow = sb("xrow", [P, TT, D])
        xb = sb("xb", [P, TT, D])
        qk = sb("qk", [P, 2, DC, T])
        sq = sb("sq", [P, 2, DC, T])
        halfn = sb("halfn", [P, 2, TT, H])
        va = sb("va", [P, TT, H, DV])
        phi = sb("phi", [P, 2, TT, H * M])
        fmax = sb("fmax", [P, 4, H])
        shift = sb("shift", [P, 4, H])
        kvbd = sb("kvbd", [P, PAIRS, 2 * DV])
        phiqT = sb("phiqT", [P, TT, PAIRS, P])
        dena = sb("dena", [P, TT, 2, H])
        oa = sb("oa", [P, TT, D])
        oaT = sb("oaT", [P, TT, DC, P])
        y1 = sb("y1", [P, TT, D])
        st1 = sb("st1", [P, TT, 6])
        mv1 = sb("mv1", [P, TT, 2])
        rs1 = sb("rs1", [P, TT])
        x1 = sb("x1", [P, TT, D])
        x1T = sb("x1T", [P, TT, DC, P])
        x1b = sb("x1b", [P, TT, D])
        qc = sb("qc", [P, TT * D])
        qs = sb("qs", [P, TT * D])
        qr = sb("qr", [P, TT * D])
        qT = sb("qT", [P, DC, T])
        ktbd = sb("ktbd", [P, DC, 4, LK])
        vcur = sb("vcur", [LK, H, DV])
        smax = sb("smax", [P, 4, 8])
        pr = sb("pr", [P, 4, 8 * LK])
        prT = sb("prT", [LK, 2, 4, P])
        denb = sb("denb", [P, TT, H])
        ob = sb("ob", [P, TT, D])
        obT = sb("obT", [P, TT, DC, P])
        y2 = sb("y2", [P, TT, D])
        st2 = sb("st2", [P, TT, 6])
        mv2 = sb("mv2", [P, TT, 2])
        rs2 = sb("rs2", [P, TT])
        x2 = sb("x2", [P, 2, TT, D])[:, 0]
        x2T = sb("x2T", [P, TT, DC, P])
        x2c = sb("x2c", [P, TT, D])
        th = sb("th", [P, T])
        h2 = sb("h2", [P, T])
        z1 = sb("z1", [P, T])
        z = sb("z", [P, T])
        stz = sb("stz", [P, TT, 6])
        mvz = sb("mvz", [P, TT, 2])
        rsz = sb("rsz", [P, TT])
        y3 = sb("y3", [P, TT, D])
        st3 = sb("st3", [P, TT, 6])
        mv3 = sb("mv3", [P, TT, 2])
        rs3 = sb("rs3", [P, TT])
        x3 = sb("x3", [P, TT, D])

        L = {n: sem("load_" + n) for n in ("cst", "qkw", "proj", "va", "oa", "ctx", "kx", "vx", "xq", "xo", "cols", "ffn")}
        x_loaded = sem("x_loaded")
        zeroed = sem("zeroed")
        pre_pe, pre_dve, pre_act, pre_pool = sem("pre_pe"), sem("pre_dve"), sem("pre_act"), sem("pre_pool")
        k_mm, k_out, q_mm, q_out = sem("k_mm"), sem("k_out"), sem("q_mm"), sem("q_out")
        n_mm, n_out, v_mm, v_out = sem("n_mm"), sem("n_out"), sem("v_mm"), sem("v_out")
        f_mm, f_max, f_shift, f_sub, f_exp, f_eps = (sem(n) for n in ("f_mm", "f_max", "f_shift", "f_sub", "f_exp", "f_eps"))
        kv_mm, kv_out = sem("kv_mm"), sem("kv_out")
        ft_mm, ft_out, num_mm, den_a, rec_a, o_a = (sem(n) for n in ("ft_mm", "ft_out", "num_mm", "den_a", "rec_a", "o_a"))
        oaT_mm, oaT_out, wo_mm, y1_sum, xb_done = (sem(n) for n in ("oaT_mm", "oaT_out", "wo_mm", "y1_sum", "xb_done"))
        st1_s, mv1_s, rs1_s, x1_s = (sem(n) for n in ("st1_s", "mv1_s", "rs1_s", "x1_s"))
        x1T_mm, x1T_out, x1b_s, xq_mm, rope_m, rope_s = (sem(n) for n in ("x1T_mm", "x1T_out", "x1b_s", "xq_mm", "rope_m", "rope_s"))
        qT_mm, qT_out, ktbd_s, vcur_s = (sem(n) for n in ("qT_mm", "qT_out", "ktbd_s", "vcur_s"))
        s_mm, s_max, s_sub, s_exp, pt_mm, pt_out, av_mm = (sem(n) for n in ("s_mm", "s_max", "s_sub", "s_exp", "pt_mm", "pt_out", "av_mm"))
        den_b, o_b, obT_mm, obT_out, wx_mm, y2_sum = (sem(n) for n in ("den_b", "o_b", "obT_mm", "obT_out", "wx_mm", "y2_sum"))
        st2_s, mv2_s, rs2_s, x2_s, x2_stored = (sem(n) for n in ("st2_s", "mv2_s", "rs2_s", "x2_s", "x2_stored"))
        x2T_mm, x2T_out, x2c_s, h_mm, h_act, z1_s, z_s = (sem(n) for n in ("x2T_mm", "x2T_out", "x2c_s", "h_mm", "h_act", "z1_s", "z_s"))
        zT_mm, stz_s, mvz_s, rsz_s, c_mm, y3_sum = (sem(n) for n in ("zT_mm", "stz_s", "mvz_s", "rsz_s", "c_mm", "y3_sum"))
        st3_s, mv3_s, rs3_s, x3_s, out_stored = (sem(n) for n in ("st3_s", "mv3_s", "rs3_s", "x3_s", "out_stored"))

        def steps(eng, step):
            step(0, None, None)
            step(1, 0, None)
            step(2, 1, 0)
            with eng.Fori(3, B) as i:
                step(i, i - 1, i - 2)
            step(None, B - 1, B - 2)
            step(None, None, B - 1)

        hb1 = sb("hb1", [P, 1])
        flat = lambda t, letters: t[:].rearrange("p %s -> p (%s)" % (letters, letters))
        spare = {"phi": flat(phi, "w t f"), "phiqT": flat(phiqT, "t q k"), "weights": flat(weights, "n c d"),
                 "ctxT": flat(ctxT, "c k"), "ktt": flat(ktt, "h r k"), "ktr": flat(ktr, "c k"),
                 "pr": flat(pr, "u k"), "sq": flat(sq, "w c t"), "qk": flat(qk, "w c t")}
        D_ = stage_d(nc, sb, spare, sem, g, x2_dram, out, (PX, PA, PS, PT, PB, PC), ones, minus_half, cst, rows, x2_stored, out_stored, zeroed)

        block = ctx.enter_context(nc.Block())

        @block.sync
        def _(sp):
            def load_x(b):
                if not (isinstance(b, int) and b == 0):
                    after(sp, v_mm, 1, b - 1, 1)
                    after(sp, xb_done, 1, b - 1, 1)
                sp.dma_start(xT[:], g["xT"][b]).then_inc(x_loaded, 16)
                sp.dma_start(xrow[:], g["x"][b].rearrange("(t p) d -> p t d", p=P)).then_inc(x_loaded, 16)

            sp.dma_start(w["ak"], g["w_ak"]).then_inc(L["qkw"], 16)
            load_x(0)
            sp.dma_start(w["aq"], g["w_aq"]).then_inc(L["qkw"], 16)
            D_.index_loads(sp)
            sp.dma_start(w["av"], g["w_av"]).then_inc(L["va"], 16)
            sp.dma_start(ctxT[:], g["ctxT"]).then_inc(L["ctx"], 16)
            sp.dma_start(w["xk"], g["w_xk"]).then_inc(L["kx"], 16)
            sp.dma_start(w["xkr"], g["w_xkr"]).then_inc(L["kx"], 16)
            sp.dma_start(w["ao"], g["w_ao"]).then_inc(L["oa"], 16)
            sp.dma_start(bo_a[:], g["bo_a"].to_broadcast([P, D])).then_inc(L["oa"], 16)
            sp.dma_start(w["xv"], g["w_xv"]).then_inc(L["vx"], 16)
            sp.dma_start(w["xq"], g["w_xq"]).then_inc(L["xq"], 16)
            sp.dma_start(w["xo"], g["w_xo"]).then_inc(L["xo"], 16)
            sp.dma_start(w["s12"], g["w_s12"]).then_inc(L["ffn"], 16)
            sp.dma_start(w3s[:], g["w3s"]).then_inc(L["ffn"], 16)
            D_.loads(sp)

            def step(a, b, c):
                if a is not None and not (isinstance(a, int) and a == B - 1):
                    load_x(a + 1)
                if c is not None:
                    after(sp, x3_s, TT, c, TT)
                    sp.dma_start(out[c].rearrange("(t p) d -> p t d", p=P), x3[:]).then_inc(out_stored, 16)
                if b is not None:
                    after(sp, x2_s, TT, b, TT)
                    sp.dma_start(x2_dram.rearrange("(b t p) d -> b p t d", b=B, p=P)[b], x2[:]).then_inc(x2_stored, 16)

            step(0, None, None)
            step(1, 0, None)
            step(2, 1, 0)
            with sp.Fori(3, B - 1) as i:
                step(i, i - 1, i - 2)
            step(B - 1, B - 2, B - 3)
            step(None, B - 1, B - 2)
            step(None, None, B - 1)
            D_.more_loads(sp)
            sp.wait_ge(x2_stored, 16 * B)
            sp.wait_ge(out_stored, 16 * B)

        @block.tensor
        def _(pe):
            def mm(o, l, r, start=True, stop=True):
                return nc.tensor.matmul(o, l, r, start=start, stop=stop)

            def project(o, lhs, rhs, n):
                for c in range(n):
                    last = mm(o, lhs(c), rhs(c), c == 0, c == n - 1)
                return last

            def pre_keys(c, hb):
                n = CT // 2
                i = 2 * c + hb
                banks = ((PS[:, 0:512], PS[:, 512:1024]), (PT[:], PB[:]))[hb]
                if i == 0:
                    pe.wait_ge(L["ctx"], 16)
                    pe.wait_ge(L["kx"], 32)
                if c == 1:
                    pe.wait_ge(pre_dve, 2 * hb + 2 + 2)
                for r, name in enumerate(("xk", "xkr")):
                    last = project(banks[r][:, 0:n], lambda d: w[name][:, d, c * P:(c + 1) * P],
                                   lambda d: ctxT[:, d, hb * n:(hb + 1) * n], DC)
                last.then_inc(pre_pe, 1)

            def pre_values(b):
                if b == 0:
                    pe.wait_ge(L["vx"], 16)
                    pe.wait_ge(pre_dve, 2 + 8)
                if b == 1:
                    pe.wait_ge(n_out, 1)
                if b >= 2:
                    pe.wait_ge(pre_act, b - 1)
                project((PT, PC)[b % 2][0:LK, 0:D], lambda d: ctxT[:, d, b * LK:(b + 1) * LK],
                        lambda d: w["xv"][:, d, :], DC).then_inc(pre_pe, 1)

            def pre_bias():
                pe.wait_ge(pre_act, B)
                pe.wait_ge(L["xo"], 16)
                for c in range(DC):
                    mm(PB[:, 0:D], cols[:, BV + c:BV + c + 1].to_broadcast([P, P]), w["xo"][:, c, :], c == 0, False)
                mm(PB[:, 0:D], ones[0:1, :], rows[:, 0, :], False, True).then_inc(pre_pe, 1)
                pe.wait_ge(L["ffn"], 32)
                mm(PB[:, D:2 * D], cols[:, SLB:SLB + 1].to_broadcast([P, P]), w3s[:], True, False)
                mm(PB[:, D:2 * D], ones[0:1, :], rows[:, 1, :], False, True).then_inc(pre_pe, 1)
                pe.wait_ge(pre_pool, 5)
                mm(PC[:, 0:D], center, w3g[:]).then_inc(pre_pe, 1)

            def kq_proj(b, which, weights, done):
                if which == 0:
                    after(pe, x_loaded, 32, b, 32)
                    after(pe, ft_out, 2, b - 1, 2)
                for c in range(DC):
                    last = project(PX[:, 512 * which + c * T:512 * which + (c + 1) * T], lambda d: weights[:, d, c * P:(c + 1) * P],
                                   lambda d: xT[:, d, :], DC)
                last.then_inc(done, 1)

            def norms(b):
                after(pe, y3_sum, TT, b - 3, TT)
                for which in range(2):
                    for t in range(TT):
                        for c in range(DC):
                            o = ((which * TT + t) * DC + c) * HC
                            last = mm(PC[:, o:o + HC], sq[:, which, c, t * P:(t + 1) * P], half_blocks)
                last.then_inc(n_mm, 1)

            def features(b, u):
                if u > 0:
                    after(pe, f_sub, 4, b, u)
                else:
                    after(pe, q_out, 2, b, 2)
                for c in range(DC):
                    last = mm(PX[:, c * 512:(c + 1) * 512], qk[:, u // 2, c, (u % 2) * P:(u % 2 + 1) * P], projbd[:, c, :])
                last.then_inc(f_mm, 1)

            def values(b):
                after(pe, y1_sum, 1, b - 1, 1)
                for t in range(TT):
                    last = project(PA[:, t * D:(t + 1) * D], lambda d: xT[:, d, t * P:(t + 1) * P],
                                   lambda d: w["av"][:, d, :], DC)
                last.then_inc(v_mm, 1)

            def kv(b, part):
                if part == 0:
                    after(pe, v_out, 1, b, 1)
                    after(pe, f_eps, 2, b, 2)
                for p in range(part * PAIRS // 4, (part + 1) * PAIRS // 4):
                    for t in range(TT):
                        last = mm(PA[:, p * 2 * DV:(p + 1) * 2 * DV], phi[:, 0, t, p * P:(p + 1) * P],
                                  va[:, t, 2 * p:2 * p + 2, :], t == 0, t == TT - 1)
                if part == 3:
                    last.then_inc(kv_mm, 1)

            def features_T(b, t):
                after(pe, f_exp, 4, b, 3 + t)
                if t == 0:
                    after(pe, f_sub, 4, b, 4)
                else:
                    after(pe, ft_out, 2, b, 1)
                for p in range(PAIRS):
                    last = nc.tensor.transpose(PX[:, p * P:(p + 1) * P], phi[:, 1, t, p * P:(p + 1) * P], ident)
                last.then_inc(ft_mm, 1)

            def numerators(b, t):
                after(pe, ft_out, 2, b, t + 1)
                if t == 0:
                    after(pe, kv_out, 2, b, 2)
                else:
                    after(pe, o_a, 2, b, 1)
                for p in range(PAIRS):
                    last = mm(PA[:, p * 2 * DV:(p + 1) * 2 * DV], phiqT[:, t, p, :], kvbd[:, p, :])
                last.then_inc(num_mm, 1)

            def transpose_rows(dst, src):
                for t in range(TT):
                    for c in range(DC):
                        last = nc.tensor.transpose(dst[:, (t * DC + c) * P:(t * DC + c + 1) * P],
                                                   src[:, t, c * P:(c + 1) * P], ident)
                return last

            def rows_times(dst, srcT, weights):
                for t in range(TT):
                    last = project(dst[:, t * D:(t + 1) * D], lambda d: srcT[:, t, d, :], lambda d: weights[:, d, :], DC)
                return last

            def scores(b, u):
                t, c = u // 2, u % 2
                if u == 0:
                    after(pe, qT_out, 1, b, 1)
                    after(pe, ktbd_s, 1, b, 1)
                    after(pe, s_sub, 4, b - 1, 4)
                else:
                    after(pe, s_sub, 4, b, u)
                for s in range(2):
                    last = mm(PS[:, 512 * s:512 * s + 4 * LK], qT[64 * s:64 * s + 64, c, t * P:(t + 1) * P],
                              ktbd[64 * s:64 * s + 64, c, :, :])
                last.then_inc(s_mm, 1)

            def probs_T(b, u, s):
                n = 2 * u + s
                if s == 0:
                    after(pe, s_exp, 4, b, u + 1)
                if n == 0:
                    after(pe, pt_out, 8, b - 1, 8)
                else:
                    after(pe, pt_out, 8, b, n)
                for j in range(4):
                    k = 4 * s + j
                    last = nc.tensor.transpose(PT[0:LK, j * P:(j + 1) * P], pr[:, u, k * LK:(k + 1) * LK], ident)
                last.then_inc(pt_mm, 1)

            def weigh_values(b, u, s):
                n = 2 * u + s
                after(pe, pt_out, 8, b, n + 1)
                if n == 0:
                    after(pe, vcur_s, 1, b, 1)
                    after(pe, qT_out, 1, b, 1)
                if n == 4:
                    after(pe, o_b, 2, b, 1)
                for j in range(4):
                    h = 8 * (u % 2) + 4 * s + j
                    last = mm(PB[:, h * DV:(h + 1) * DV], prT[:, s, j, :], vcur[:, h, :])
                last.then_inc(av_mm, 1)

            def step(a, b, c):
                A, Bb, Cc = a is not None, b is not None, c is not None
                first = isinstance(a, int) and a == 0
                if A:
                    if first:
                        pe.wait_ge(L["qkw"], 16)
                    kq_proj(a, 0, w["ak"], k_mm)
                if Cc:
                    weigh_values(c, 3, 1)
                if Bb:
                    numerators(b, 1)
                if A:
                    if first:
                        pe.wait_ge(L["qkw"], 32)
                    kq_proj(a, 1, w["aq"], q_mm)
                if Bb:
                    after(pe, o_a, 2, b, 2)
                    transpose_rows(PA, oa).then_inc(oaT_mm, 1)
                if Cc:
                    after(pe, o_b, 2, c, 2)
                    transpose_rows(PB, ob).then_inc(obT_mm, 1)
                if Bb:
                    after(pe, oaT_out, 1, b, 1)
                    if isinstance(b, int) and b == 0:
                        pe.wait_ge(L["oa"], 32)
                    rows_times(PA, oaT, w["ao"]).then_inc(wo_mm, 1)
                if A:
                    if first:
                        pe.wait_ge(L["proj"], 16 * 8)
                    features(a, 0)
                if Cc:
                    after(pe, obT_out, 1, c, 1)
                    rows_times(PB, obT, w["xo"]).then_inc(wx_mm, 1)
                if A:
                    if first:
                        pe.wait_ge(L["cst"], 16)
                    if isinstance(a, int) and a == 1:
                        pe.wait_ge(pre_dve, 13)
                    norms(a)
                if Bb:
                    after(pe, x1_s, TT, b, TT)
                    after(pe, y2_sum, 1, b - 1, 1)
                    if isinstance(b, int) and b == 0:
                        pe.wait_ge(pre_dve, 13)
                    transpose_rows(PB, x1).then_inc(x1T_mm, 1)
                if A:
                    if first:
                        pe.wait_ge(L["va"], 16)
                    values(a)
                if first:
                    pe.wait_ge(L["cols"], 32)
                    pre_keys(0, 0)
                    pre_keys(0, 1)
                if A:
                    features(a, 1)
                if first:
                    pre_keys(1, 0)
                    pre_keys(1, 1)
                if Cc:
                    after(pe, x2_s, TT, c, TT)
                    if A:
                        after(pe, n_out, 1, a, 1)
                    after(pe, y3_sum, TT, c - 1, TT)
                    transpose_rows(PC, x2).then_inc(x2T_mm, 1)
                if Bb:
                    after(pe, x1T_out, 1, b, 1)
                    if isinstance(b, int) and b == 0:
                        pe.wait_ge(L["xq"], 16)
                    rows_times(PB, x1T, w["xq"]).then_inc(xq_mm, 1)
                if A:
                    features(a, 2)
                if Bb:
                    after(pe, rope_s, 1, b, 1)
                    for t in range(TT):
                        for d in range(DC):
                            last = nc.tensor.transpose(PB[:, d * T + t * P:d * T + (t + 1) * P],
                                                       qr[:, t * D + d * P:t * D + (d + 1) * P], ident)
                    last.then_inc(qT_mm, 1)
                if A:
                    kv(a, 0)
                if Bb:
                    scores(b, 0)
                if Cc:
                    after(pe, x2T_out, 1, c, 1)
                    for r in range(2):
                        last = project(PC[:, r * T:(r + 1) * T], lambda d: w["s12"][:, d, r * FH:(r + 1) * FH],
                                       lambda d: x2T[:, :, d, :], DC)
                    last.then_inc(h_mm, 1)
                if first:
                    for n in range(B // 2):
                        pre_values(n)
                if A:
                    kv(a, 1)
                if Bb:
                    probs_T(b, 0, 0)
                    scores(b, 1)
                if A:
                    kv(a, 2)
                if Bb:
                    probs_T(b, 0, 1)
                if A:
                    features(a, 3)
                if Bb:
                    weigh_values(b, 0, 0)
                if Cc:
                    after(pe, z_s, 1, c, 1)
                    after(pe, h_act, 2, c, 2)
                    for t in range(TT):
                        last = nc.tensor.transpose(PC[:, t * FH:(t + 1) * FH], z[:, t * P:(t + 1) * P], ident)
                    last.then_inc(zT_mm, 1)
                if first:
                    for n in range(B // 2, B):
                        pre_values(n)
                if Bb:
                    weigh_values(b, 0, 1)
                    probs_T(b, 1, 0)
                    scores(b, 2)
                if A:
                    kv(a, 3)
                if Bb:
                    probs_T(b, 1, 1)
                    weigh_values(b, 1, 0)
                if A:
                    features_T(a, 0)
                if Bb:
                    weigh_values(b, 1, 1)
                    probs_T(b, 2, 0)
                if Bb:
                    scores(b, 3)
                    probs_T(b, 2, 1)
                    weigh_values(b, 2, 0)
                if first:
                    pre_bias()
                if A:
                    numerators(a, 0)
                if Cc:
                    after(pe, stz_s, TT, c, TT)
                    for t in range(TT):
                        last = mm(PC[:, t * D:(t + 1) * D], z[:, t * P:(t + 1) * P], w3c_s[:])
                    last.then_inc(c_mm, 1)
                if Bb:
                    weigh_values(b, 2, 1)
                    probs_T(b, 3, 0)
                if A:
                    features_T(a, 1)
                if Bb:
                    probs_T(b, 3, 1)
                    weigh_values(b, 3, 0)
                if Bb and not A:
                    pe.wait_ge(y1_sum, B)
                    D_.prep_tensor(pe)

            steps(pe, step)
            D_.tensor(pe)

        @block.scalar
        def _(act):
            def cp(o, i, s=1.0):
                return nc.scalar.activation(o, i, ACT.Copy, scale=s)

            def out_of(b, mm_s, per, k, o, i, done):
                after(act, mm_s, per, b, k)
                cp(o, i).then_inc(done, 1)

            def kq(b, which, mm_s, done):
                after(act, mm_s, 1, b, 1)
                after(act, f_mm, 4, b - 1, 2 * which + 2)
                after(act, n_mm, 1, b - 1, 1)
                flat = "p c t -> p (c t)"
                bank = PX[:, 512 * which:512 * (which + 1)]
                cp(qk[:, which].rearrange(flat), bank, SCALE).then_inc(done, 1)
                nc.scalar.activation(sq[:, which].rearrange(flat), bank, ACT.Square, scale=SCALE).then_inc(done, 1)

            def f_exponent(b, u):
                after(act, f_sub, 4, b, u + 1)
                f = phi[:, u // 2, u % 2, :]
                nc.scalar.activation(f, f, ACT.Exp).then_inc(f_exp, 1)
                if u < 2:
                    after(act, f_exp, 4, b, u + 1)
                    nc.scalar.activation(f, f, ACT.Copy, bias=EPS_PHI).then_inc(f_eps, 1)

            def s_exponent(b, u):
                after(act, s_sub, 4, b, u + 1)
                nc.scalar.activation(pr[:, u, :], pr[:, u, :], ACT.Exp, scale=SCALE).then_inc(s_exp, 1)

            def pt(b, n):
                s = n % 2
                after(act, pt_mm, 8, b, n + 1)
                if n >= 2:
                    after(act, av_mm, 8, b, n - 1)
                else:
                    after(act, av_mm, 8, b - 1, 7 + n)
                cp(prT[:, s].rearrange("k j t -> k (j t)"), PT[0:LK, :]).then_inc(pt_out, 1)

            def ft(b, t):
                after(act, ft_mm, 2, b, t + 1)
                after(act, num_mm, 2, b - 1, t + 1)
                nc.scalar.activation(phiqT[:, t].rearrange("p q t -> p (q t)"), PX[:], ACT.Copy,
                                     bias=EPS_PHI).then_inc(ft_out, 1)

            def pre_value(b):
                if b == 0:
                    act.wait_ge(zeroed, 5)
                act.wait_ge(pre_pe, 4 + b + 1)
                cp(vx[:, b, :, 0:DK], (PT, PC)[b % 2][0:LK, 0:D].rearrange("p (h k) -> p h k", k=DK)).then_inc(pre_act, 1)

            def step(a, b, c):
                A, Bb, Cc = a is not None, b is not None, c is not None
                first = isinstance(a, int) and a == 0
                if A:
                    kq(a, 0, k_mm, k_out)
                if A:
                    kq(a, 1, q_mm, q_out)
                if Cc:
                    after(act, wx_mm, 1, c - 1, 1)
                    out_of(c, obT_mm, 1, 1, obT[:].rearrange("p t c q -> p (t c q)"), PB[:], obT_out)
                if A:
                    after(act, v_mm, 1, a, 1)
                    after(act, kv_mm, 1, a - 1, 1)
                    if first:
                        act.wait_ge(zeroed, 4)
                    cp(va[:, :, :, 0:DK].rearrange("p t h k -> p (t h) k"),
                       PA[:].rearrange("p (g k) -> p g k", k=DK)).then_inc(v_out, 1)
                if Bb:
                    after(act, xq_mm, 1, b - 1, 1)
                    out_of(b, x1T_mm, 1, 1, x1T[:].rearrange("p t c q -> p (t c q)"), PB[:], x1T_out)
                if A:
                    f_exponent(a, 0)
                if Cc:
                    after(act, h_mm, 1, c - 1, 1)
                    out_of(c, x2T_mm, 1, 1, x2T[:].rearrange("p t c q -> p (t c q)"), PC[:], x2T_out)
                if A:
                    f_exponent(a, 1)
                if Bb:
                    s_exponent(b, 0)
                if Cc:
                    after(act, h_mm, 1, c, 1)
                    after(act, z_s, 1, c - 1, 1)
                    if isinstance(c, int) and c == 0:
                        act.wait_ge(pre_pool, 6)
                    nc.scalar.activation(th[:], PC[:, 0:T], ACT.Tanh, bias=hb1[:], scale=0.5).then_inc(h_act, 1)
                    nc.scalar.activation(h2[:], PC[:, T:2 * T], ACT.Identity, bias=cols[:, SB2:SB2 + 1]).then_inc(h_act, 1)
                if first:
                    for n in range(B // 2):
                        pre_value(n)
                if Bb:
                    pt(b, 0)
                if A:
                    f_exponent(a, 2)
                if Bb:
                    pt(b, 1)
                    s_exponent(b, 1)
                    pt(b, 2)
                if A:
                    f_exponent(a, 3)
                if first:
                    for n in range(B // 2, B):
                        pre_value(n)
                if Bb:
                    pt(b, 3)
                    s_exponent(b, 2)
                if A:
                    ft(a, 0)
                if Bb:
                    pt(b, 4)
                    pt(b, 5)
                    s_exponent(b, 3)
                    pt(b, 6)
                if A:
                    ft(a, 1)
                if Bb:
                    pt(b, 7)
                if Bb and not A:
                    D_.prep_scalar(act)

            act.dma_start(cst[:], g["cst"]).then_inc(L["cst"], 16)
            act.dma_start(cols[:], g["cols"]).then_inc(L["cols"], 16)
            act.dma_start(rows[:], g["rows"]).then_inc(L["cols"], 16)
            act.wait_ge(zeroed, 2)
            for h in range(HC):
                act.dma_start(projbd[h * DK:(h + 1) * DK, :, h * M:(h + 1) * M], g["proj"][h]).then_inc(L["proj"], 16)
            act.wait_ge(L["cols"], 32)
            steps(act, step)
            D_.scalar(act)


        @block.vector
        def _(dve):
            tt, tsc, stt = nc.vector.tensor_tensor, nc.vector.tensor_scalar, nc.vector.scalar_tensor_tensor

            def f_maximum(b, u):
                after(dve, f_mm, 4, b, u + 1)
                after(dve, f_shift, 4, b - 1, u + 1)
                nc.vector.tensor_reduce(fmax[:, u, :], PX[:].rearrange("p (h m) -> p h m", m=M), AX_X, ALU.max).then_inc(f_max, 1)

            def f_subtract(b, u):
                after(dve, f_max, 4, b, u + 1)
                after(dve, n_out, 1, b, 1)
                after(dve, f_sub, 4, b - 1, u + 1)
                tt(shift[:, u, :], fmax[:, u, :], halfn[:, u // 2, u % 2, :], ALU.add).then_inc(f_shift, 1)
                after(dve, f_shift, 4, b, u + 1)
                if u < 2:
                    after(dve, kv_mm, 1, b - 1, 1)
                else:
                    after(dve, ft_mm, 2, b - 1, u - 1)
                tt(phi[:, u // 2, u % 2, :].rearrange("p (h m) -> p h m", m=M), PX[:].rearrange("p (h m) -> p h m", m=M),
                   shift[:, u, :].unsqueeze(2).to_broadcast([P, H, M]), ALU.subtract).then_inc(f_sub, 1)

            def banks(ap):
                return ap.rearrange("p (s f) -> p s f", s=2)[:, :, 0:4 * LK].rearrange("p s (j k) -> p s j k", k=LK)

            def s_maximum(b, u):
                after(dve, s_mm, 4, b, u + 1)
                after(dve, s_sub, 4, b - 1, u + 1)
                nc.vector.tensor_reduce(smax[:, u, :].rearrange("p (s j) -> p s j", s=2), banks(PS[:]), AX_X, ALU.max).then_inc(s_max, 1)

            def s_subtract(b, u):
                after(dve, s_max, 4, b, u + 1)
                after(dve, pt_mm, 8, b - 1, 2 * u + 2)
                tt(pr[:, u, :].rearrange("p (s j k) -> p s j k", s=2, k=LK), banks(PS[:]),
                   smax[:, u, :].rearrange("p (s j) -> p s j", s=2).unsqueeze(3).to_broadcast([P, 2, 4, LK]),
                   ALU.subtract).then_inc(s_sub, 1)

            def heads(ap):
                return ap[:, 0:H * DV].rearrange("p (h k) -> p h k", k=DV)

            def norm_a(b, t):
                after(dve, num_mm, 2, b, t + 1)
                after(dve, rec_a, 2, b - 1, t + 1)
                tsc(dena[:, t, 0, :], heads(PA[:])[:, :, DK], M * EPS_PHI, None, ALU.add).then_inc(den_a, 1)
                after(dve, den_a, 2, b, t + 1)
                after(dve, o_a, 2, b - 1, t + 1)
                nc.vector.reciprocal(dena[:, t, 1, :], dena[:, t, 0, :]).then_inc(rec_a, 1)
                after(dve, rec_a, 2, b, t + 1)
                after(dve, oaT_mm, 1, b - 1, 1)
                tt(oa[:, t, :].rearrange("p (h k) -> p h k", k=DK), heads(PA[:])[:, :, 0:DK],
                   dena[:, t, 1, :].unsqueeze(2).to_broadcast([P, H, DK]), ALU.mult).then_inc(o_a, 1)

            def norm_b(b, t):
                after(dve, av_mm, 8, b, 4 * t + 4)
                after(dve, o_b, 2, b - 1, t + 1)
                nc.vector.reciprocal(denb[:, t, :], heads(PB[:])[:, :, DK]).then_inc(den_b, 1)
                after(dve, den_b, 2, b, t + 1)
                after(dve, obT_mm, 1, b - 1, 1)
                tt(ob[:, t, :].rearrange("p (h k) -> p h k", k=DK), heads(PB[:])[:, :, 0:DK],
                   denb[:, t, :].unsqueeze(2).to_broadcast([P, H, DK]), ALU.mult).then_inc(o_b, 1)

            def statistics(b, y, st, mv, st_s, mv_s, rs_s):
                after(dve, mv_s, TT, b - 1, TT)
                after(dve, rs_s, 2, b - 1, 2)
                for t in range(TT):
                    nc.vector.bn_stats(st[:, t, :], y(t)).then_inc(st_s, 1)
                for t in range(TT):
                    after_plainly(dve, zeroed, (st_s, TT, b, t + 1))
                    nc.vector.bn_aggr(mv[:, t, :], st[:, t, :]).then_inc(mv_s, 1)

            def normalize(b, y, mv, rs, rs_s, x, x_s):
                after(dve, rs_s, 2, b, 2)
                for t in range(TT):
                    tsc(x[:, t, :], y[:, t, :], mv[:, t, 0:1], rs[:, t:t + 1], ALU.subtract, ALU.mult).then_inc(x_s, 1)

            def pre_queries():
                dve.wait_ge(L["cst"], 16)
                dve.wait_ge(L["cols"], 32)
                for c in range(DC):
                    tsc(rq_tmp[:, c, :], cosT, cols[:, BQ + c:BQ + c + 1], None, ALU.mult).then_inc(pre_dve, 1)
                dve.wait_ge(pre_dve, 2)
                for c in range(DC):
                    stt(out=rbqT[:, c, :], in0=sinT, scalar=cols[:, BQR + c:BQR + c + 1], in1=rq_tmp[:, c, :],
                        op0=ALU.mult, op1=ALU.add)

            def pre_keys(i):
                c, hb = i // 2, i % 2
                n = B // 2
                dve.wait_ge(pre_pe, i + 1)
                if i >= 2:
                    dve.wait_ge(pre_pool, i - 1)
                banks = ((PS[:, 0:512], PS[:, 512:1024]), (PT[:], PB[:]))[hb]
                for r, (bias, table) in enumerate(((BK, cosk), (BKR, sink))):
                    stt(out=ktt[:, hb, r, :].rearrange("p (b k) -> p b k", k=LK),
                        in0=banks[r][:, 0:n * LK].rearrange("p (b k) -> p b k", k=LK),
                        scalar=cols[:, bias + c:bias + c + 1], in1=table.unsqueeze(1).to_broadcast([P, n, LK]),
                        op0=ALU.add, op1=ALU.mult).then_inc(pre_dve, 1)

            def pre_bias():
                dve.wait_ge(pre_pe, 4 + B + 2)
                nc.vector.tensor_copy(bo_b[:], PB[:, 0:D]).then_inc(pre_dve, 1)
                nc.vector.tensor_copy(c3_s[:], PB[:, D:2 * D]).then_inc(pre_dve, 1)
                dve.wait_ge(pre_pe, 4 + B + 3)
                nc.vector.tensor_copy(w3c_s[:], PC[:, 0:D]).then_inc(pre_dve, 1)

            def step(a, b, c):
                A, Bb, Cc = a is not None, b is not None, c is not None
                first = isinstance(a, int) and a == 0
                if Cc:
                    norm_b(c, 1)
                if Bb:
                    norm_a(b, 1)
                    after(dve, oaT_mm, 1, b, 1)
                    after(dve, wo_mm, 1, b - 1, 1)
                    nc.vector.tensor_copy(oaT[:].rearrange("p t c q -> p (t c q)"), PA[:]).then_inc(oaT_out, 1)
                    after(dve, wo_mm, 1, b, 1)
                    after(dve, xb_done, 1, b, 1)
                    after(dve, x1_s, TT, b - 1, TT)
                    tt(y1[:].rearrange("p t d -> p (t d)"), PA[:], xb[:].rearrange("p t d -> p (t d)"), ALU.add).then_inc(y1_sum, 1)
                    after(dve, y1_sum, 1, b, 1)
                    statistics(b, lambda t: y1[:, t, :], st1, mv1, st1_s, mv1_s, rs1_s)
                if A:
                    f_maximum(a, 0)
                if Bb:
                    after(dve, x1T_mm, 1, b - 1, 1)
                    after(dve, x1b_s, 1, b - 1, 1)
                    normalize(b, y1, mv1, rs1, rs1_s, x1, x1_s)
                if Cc:
                    after(dve, wx_mm, 1, c, 1)
                    after(dve, x1b_s, 1, c, 1)
                    after(dve, x2_s, TT, c - 1, TT)
                    tt(y2[:].rearrange("p t d -> p (t d)"), PB[:], x1b[:].rearrange("p t d -> p (t d)"), ALU.add).then_inc(y2_sum, 1)
                    after(dve, y2_sum, 1, c, 1)
                    statistics(c, lambda t: y2[:, t, :], st2, mv2, st2_s, mv2_s, rs2_s)
                if A:
                    after(dve, n_mm, 1, a, 1)
                    after(dve, f_shift, 4, a - 1, 4)
                    nc.vector.tensor_copy(halfn[:].rearrange("p w t h -> p (w t h)"), PC[:, 0:4 * H]).then_inc(n_out, 1)
                    f_subtract(a, 0)
                if first:
                    pre_keys(0)
                    pre_keys(1)
                if Cc:
                    after(dve, x2T_mm, 1, c - 1, 1)
                    after(dve, x2c_s, 1, c - 1, 1)
                    after(dve, x2_stored, 16, c - 1, 16)
                    normalize(c, y2, mv2, rs2, rs2_s, x2, x2_s)
                if A:
                    f_maximum(a, 1)
                    f_subtract(a, 1)
                if first:
                    pre_keys(2)
                    pre_keys(3)
                if Bb:
                    after(dve, xq_mm, 1, b, 1)
                    after(dve, rope_s, 1, b - 1, 1)
                    tt(qc[:], PB[:], cosq, ALU.mult).then_inc(rope_m, 1)
                    view = lambda ap: ap.rearrange("p (g s e) -> p g s e", s=2, e=DK // 2)
                    for s in range(2):
                        tt(view(qs[:])[:, :, s, :], view(PB[:])[:, :, 1 - s, :], view(sinq)[:, :, s, :], ALU.mult).then_inc(rope_m, 1)
                    after(dve, rope_m, 3, b, 3)
                    after(dve, qT_mm, 1, b - 1, 1)
                    tt(qr[:], qc[:], qs[:], ALU.add).then_inc(rope_s, 1)
                if Bb:
                    after(dve, qT_mm, 1, b, 1)
                    after(dve, s_mm, 4, b - 1, 4)
                    tt(qT[:].rearrange("p c t -> p (c t)"), PB[:], rbqT[:].rearrange("p c t -> p (c t)"), ALU.add).then_inc(qT_out, 1)
                if A:
                    f_maximum(a, 2)
                if Bb:
                    s_maximum(b, 0)
                    s_subtract(b, 0)
                if A:
                    f_subtract(a, 2)
                if Cc:
                    after(dve, h_act, 2, c, 2)
                    after(dve, z_s, 1, c - 1, 1)
                    stt(out=z1[:], in0=PC[:, 0:T], scalar=cols[:, SB1:SB1 + 1], in1=h2[:], op0=ALU.add, op1=ALU.mult).then_inc(z1_s, 1)
                if Bb:
                    s_maximum(b, 1)
                    s_subtract(b, 1)
                if Cc:
                    after(dve, z1_s, 1, c, 1)
                    after(dve, c_mm, 1, c - 1, 1)
                    stt(out=z[:], in0=th[:], scalar=1.0, in1=z1[:], op0=ALU.add, op1=ALU.mult).then_inc(z_s, 1)
                if A:
                    f_maximum(a, 3)
                    f_subtract(a, 3)
                if Cc:
                    after(dve, zT_mm, 1, c, 1)
                    statistics(c, lambda t: PC[:, t * FH:(t + 1) * FH], stz, mvz, stz_s, mvz_s, rsz_s)
                if Bb:
                    s_maximum(b, 2)
                    s_subtract(b, 2)
                if A:
                    after(dve, kv_mm, 1, a, 1)
                    after(dve, num_mm, 2, a - 1, 2)
                    if first:
                        dve.wait_ge(zeroed, 5)
                    src = PA[:, 0:H * DV].rearrange("p (q k) -> p q k", k=2 * DV)
                    for s in range(2):
                        nc.vector.tensor_copy(kvbd[64 * s:64 * s + 64, :, s * DV:(s + 1) * DV],
                                              src[64 * s:64 * s + 64, :, s * DV:(s + 1) * DV]).then_inc(kv_out, 1)
                if Bb:
                    norm_b(b, 0)
                    s_maximum(b, 3)
                    s_subtract(b, 3)
                if first:
                    pre_bias()
                if A:
                    norm_a(a, 0)
                if Cc:
                    after(dve, c_mm, 1, c, 1)
                    after(dve, rsz_s, 2, c, 2)
                    after(dve, x2c_s, 1, c, 1)
                    after(dve, x3_s, TT, c - 1, TT)
                    for t in range(TT):
                        stt(out=y3[:, t, :], in0=PC[:, t * D:(t + 1) * D], scalar=rsz[:, t:t + 1], in1=x2c[:, t, :],
                            op0=ALU.mult, op1=ALU.add).then_inc(y3_sum, 1)
                    after(dve, y3_sum, TT, c, TT)
                    statistics(c, lambda t: y3[:, t, :], st3, mv3, st3_s, mv3_s, rs3_s)
                if Cc:
                    after(dve, out_stored, 16, c - 1, 16)
                    normalize(c, y3, mv3, rs3, rs3_s, x3, x3_s)

            D_.prep_vector(dve)
            pre_queries()
            steps(dve, step)
            D_.vector(dve)

        @block.gpsimd
        def _(pool):
            gp = nc.gpsimd

            def rstd(b, mv, mv_s, eps, rs, rs_s, last_use, per):
                after_plainly(pool, zeroed, (mv_s, TT, b, TT), (last_use, per, b - 1, per))
                gp.tensor_scalar(rs[:], mv[:, :, 1], eps, 1.0, ALU.add, ALU.mult).then_inc(rs_s, 1)
                after(pool, rs_s, 2, b, 1)
                gp.tensor_tensor(rs[:], rs[:], minus_half[:, 0:TT], ALU.pow).then_inc(rs_s, 1)

            def add_bias(dst, src, bias, done):
                gp.tensor_tensor(dst[:], src[:], bias[:].unsqueeze(1).to_broadcast([P, TT, D]), ALU.add).then_inc(done, 1)

            def pre_keys(i):
                n, c, hb = CT // 2, i // 2, i % 2
                pool.wait_ge(pre_dve, 2 + 2 * i + 2)
                gp.tensor_tensor(ktr[:, c, hb * n:(hb + 1) * n], ktt[:, hb, 0, :], ktt[:, hb, 1, :], ALU.add).then_inc(pre_pool, 1)

            def pre_ffn():
                pool.wait_ge(L["ffn"], 32)
                gp.tensor_scalar(w3g[:], w3s[:], cols[:, SG:SG + 1], 1.0, ALU.mult, ALU.mult).then_inc(pre_pool, 1)
                gp.tensor_scalar(hb1[:], cols[:, SB1:SB1 + 1], 0.5, 0.0, ALU.mult, ALU.add).then_inc(pre_pool, 1)

            def step(a, b, c):
                A, Bb, Cc = a is not None, b is not None, c is not None
                first = isinstance(a, int) and a == 0
                if Bb:
                    after(pool, s_mm, 4, b - 1, 4)
                    for c2 in range(DC):
                        ins = gp.tensor_tensor(ktbd[:, c2, :, :],
                                               ktr[:, c2, :].rearrange("p (b k) -> p b k", b=B)[:, bass.ds(b, 1), :].to_broadcast([P, 4, LK]),
                                               head_mask.unsqueeze(2).to_broadcast([P, 4, LK]), ALU.mult)
                    ins.then_inc(ktbd_s, 1)
                    after(pool, av_mm, 8, b - 1, 8)
                    gp.tensor_copy(vcur[:].rearrange("k h e -> k (h e)"),
                                   vx[:].rearrange("k b h e -> k b (h e)")[:, bass.ds(b, 1), :].rearrange("k b f -> k (b f)")).then_inc(vcur_s, 1)
                if Bb:
                    rstd(b, mv1, mv1_s, EPS_LN, rs1, rs1_s, x1_s, TT)
                if Cc:
                    rstd(c, mv2, mv2_s, EPS_LN, rs2, rs2_s, x2_s, TT)
                if A:
                    after(pool, x_loaded, 32, a, 32)
                    after(pool, y1_sum, 1, a - 1, 1)
                    if first:
                        pool.wait_ge(L["oa"], 32)
                    add_bias(xb, xrow, bo_a, xb_done)
                if first:
                    pre_keys(0)
                    pre_keys(1)
                if Bb:
                    after(pool, x1_s, TT, b, TT)
                    after(pool, y2_sum, 1, b - 1, 1)
                    add_bias(x1b, x1, bo_b, x1b_s)
                if first:
                    pre_keys(2)
                    pre_keys(3)
                if first:
                    pre_ffn()
                    pool.wait_ge(pre_pool, 6)
                    pool.wait_ge(pre_act, B)
                    pool.wait_ge(pre_dve, 13)
                if Cc:
                    after(pool, x2_s, TT, c, TT)
                    after(pool, y3_sum, TT, c - 1, TT)
                    add_bias(x2c, x2, c3_s, x2c_s)
                if Bb and not A:
                    D_.prep_gpsimd(pool)
                if Cc:
                    rstd(c, mvz, mvz_s, 4 * EPS_LN, rsz, rsz_s, y3_sum, TT)
                    rstd(c, mv3, mv3_s, EPS_LN, rs3, rs3_s, x3_s, TT)

            gp.memset(ones[:], 1.0).then_inc(zeroed, 1)
            gp.memset(projbd[:], 0.0).then_inc(zeroed, 1)
            gp.memset(minus_half[:], -0.5).then_inc(zeroed, 1)
            gp.memset(va[:, :, :, DK:DV], 1.0)
            gp.memset(vx[:, :, :, DK:DV], 1.0).then_inc(zeroed, 1)
            gp.memset(kvbd[:], 0.0).then_inc(zeroed, 1)
            pool.wait_ge(L["cols"], 32)
            pool.wait_ge(L["cst"], 16)
            D_.prep_rows(pool)
            steps(pool, step)
            D_.gpsimd(pool)


class stage_d:

    def __init__(self, nc, sb, spare, sem, g, x2_dram, out, banks, ones, minus_half, cst, rows, x2_stored, out_stored, zeroed):
        self.nc, self.g, self.x2_dram, self.out = nc, g, x2_dram, out
        self.PX, self.PA, self.PS, self.PT, self.PB, self.PC = banks
        self.ones, self.minus_half, self.cst, self.rows = ones, minus_half, cst, rows
        self.x2_stored, self.out_stored, self.zeroed = x2_stored, out_stored, zeroed
        self.ident = cst[:, C_ID:C_ID + P]
        self.w12 = [sb(f"w12_{n}", [P, 2, DC, FH]) for n in range(2)]
        self.w3 = sb("w3_units", [P, NU, D])
        self.w3g = spare["phi"][:, 0:NU * D].rearrange("p (n d) -> p n d", n=NU)
        self.w3c = sb("w3c_units", [P, NU, D])
        self.b1 = sb("b1_units", [P, NU])
        self.hb1 = sb("hb1_units", [P, NU])
        self.b2 = sb("b2_units", [P, NU])
        self.lng = sb("lng_units", [P, NU])
        self.lnb = sb("lnb_units", [P, NU])
        self.lnb_diag = sb("lnb_diag", [P, NU, NU])
        self.b3 = sb("b3_units", [NU, D])
        self.c3 = sb("c3_units", [NU, D])
        self.gate_w = sb("gate_w", [P, DC, NU])
        self.gate_b = sb("gate_b", [1, NU])
        self.exp_bias = sb("exp_bias", [P, NE])
        W = MT + NM
        self.idx = sb("idx_int", [P, 2, W], I32)
        both = lambda name, at: spare[name][:, at:at + 2 * W].rearrange("p (k w) -> p k w", k=2)
        self.idx_f, self.idx_w, self.idx_n = (both("phi", 2 * W * j) for j in range(3))
        self.idx_c, self.idx_ok = both("pr", 0), both("pr", 2 * W)
        self.row_no = spare["phi"][:, 0:W]
        self.row_ok = spare["phi"][:, W:2 * W]
        self.row_to = sb("row_to", [P, W])
        self.same = spare["phiqT"].rearrange("p (j m) -> p j m", j=MT)
        self.dup = sb("dup", [P, MT])
        self.to_f = sb("to_f", [P, MT])
        self.src_row = sb("src_row", [P, MT], U32)
        self.dst_row = sb("dst_row", [P, MT], U32)
        rows_of = lambda name, at: spare[name][:, at:at + MT * D].rearrange("p (t d) -> p t d", t=MT)
        self.xg, self.acc, self.yo = rows_of("pr", 0), rows_of("pr", MT * D), rows_of("qk", 0)
        self.xgT = spare["sq"].rearrange("p (c m) -> p c m", c=DC)
        wide = lambda j: spare["phi"][:, j * NM:(j + 1) * NM]
        self.z1, self.z, self.th, self.h2 = ([wide(2 * j), wide(2 * j + 1)] for j in range(4))
        self.st = sb("st_d", [P, MT, 6])
        self.mv = sb("mv_d", [P, MT, 2])
        self.rs = sb("rs_d", [P, MT])
        self.alpha = [sb(f"alpha_d{n}", [P, MT]) for n in range(2)]
        self.st4 = sb("st4", [P, MT, 6])
        self.mv4 = sb("mv4", [P, MT, 2])
        self.rs4 = sb("rs4", [P, MT])
        self.sg = sb("sg", [P, MT, NU])
        self.score = sb("score", [P, MT, NU])
        self.sel = sb("sel", [P, MT, NE])
        self.top = sb("top", [P, MT])
        self.eq = sb("eq", [P, MT, NE])
        self.rank = sb("rank", [P, MT, NE])
        self.first = sb("first", [P, MT])
        self.onehot = sb("onehot", [P, MT, NE])
        self.picked = sb("picked", [P, MT, NE])
        self.tops = sb("tops", [P, MT])
        self.diff = sb("diff", [P, MT])
        self.tdiff = sb("tdiff", [P, MT])
        self.ew = sb("ew", [P, MT])
        self.ow = sb("ow", [P, MT, NU])
        self.owT = sb("owT", [NU, NM])
        n = lambda k: sem("d_" + k)
        self.loaded, self.w12_loaded = n("loaded"), [n("w12_loaded_even"), n("w12_loaded_odd")]
        self.g_w3, self.p_mm, self.p_out, self.c3_out = n("g_w3"), n("p_mm"), n("p_out"), n("c3_out")
        self.ix_loaded, self.ix, self.keep, self.scatter = n("index_loaded"), n("index"), n("keep"), n("scatter")
        self.gather = n("gather")
        self.xgT_mm, self.xgT_out, self.lg_mm, self.lg_sig = n("xgT_mm"), n("xgT_out"), n("lg_mm"), n("lg_sig")
        self.gate, self.sig2, self.owT_mm, self.owT_out, self.c_mm = n("gate"), n("sig2"), n("owT_mm"), n("owT_out"), n("c_mm")
        self.acc_0 = n("acc_0")
        self.h_mm, self.h_act, self.z1_s, self.z_s, self.zT_mm = n("h_mm"), n("h_act"), n("z1"), n("z"), n("zT_mm")
        self.st_s, self.mv_s, self.rs_s, self.al_s, self.o_mm, self.acc_s = n("st"), n("mv"), n("rs"), n("alpha"), n("o_mm"), n("acc")
        self.st4_s, self.mv4_s, self.rs4_s, self.yo_s = n("st4"), n("mv4"), n("rs4"), n("yo")

    LOADS = 9
    gather_ready, same_ready, scatter_ready = 14, 14 + MT, 14 + 2 * MT + 2
    diff_ready, gate_ready = 10, 13

    def units(self, eng, unit):
        unit(0, 0)
        unit(1, 1)
        with eng.Fori(1, NU // 2) as i:
            for k in range(2):
                unit(i * 2 + k, k)
        unit(NU - 1, 0)

    def index_loads(self, sp):
        sp.dma_start(self.idx[:, :, 0:MT], self.g["idx_cols"]).then_inc(self.ix_loaded, 16)
        sp.dma_start(self.idx[:, :, MT:], self.g["idx_rows"].to_broadcast([P, 2, NM])).then_inc(self.ix_loaded, 16)

    def loads(self, sp):
        g = self.g
        for dst, src in ((self.w3[:], g["w3_units"]), (self.b1[:], g["b1_units"]), (self.b2[:], g["b2_units"]),
                         (self.lng[:], g["lng_units"]), (self.lnb[:], g["lnb_units"]), (self.b3[:], g["b3_units"]),
                         (self.gate_w[:], g["gate_w"]), (self.gate_b[:], g["gate_b"]),
                         (self.exp_bias[:], g["exp_bias"].to_broadcast([P, NE]))):
            sp.dma_start(dst, src).then_inc(self.loaded, 16)
        for n in range(2):
            sp.dma_start(self.w12[n][:], g["w12_units"][n]).then_inc(self.w12_loaded[n], 16)

    def more_loads(self, sp):
        def load(n, k):
            if not isinstance(n, int) or n >= 2:
                after(sp, self.h_mm, 1, n - 2, 1)
                sp.dma_start(self.w12[k][:], self.g["w12_units"][n]).then_inc(self.w12_loaded[k], 16)
        self.units(sp, load)

    def prep_gpsimd(self, pool):
        gp = self.nc.gpsimd
        pool.wait_ge(self.loaded, 16 * self.LOADS)
        gp.memset(self.lnb_diag[:], 0.0).then_inc(self.g_w3, 1)
        gp.tensor_tensor(self.w3g[:], self.w3[:], self.lng[:].unsqueeze(2).to_broadcast([P, NU, D]), ALU.mult).then_inc(self.g_w3, 1)
        gp.tensor_scalar(self.hb1[:], self.b1[:], 0.5, 1.0, ALU.mult, ALU.mult).then_inc(self.g_w3, 1)
        pool.wait_ge(self.g_w3, 1)
        gp.tensor_copy(self.lnb_diag[:].rearrange("p a b -> p (a b)")[:, 0:NU * NU:NU + 1], self.lnb[:]).then_inc(self.g_w3, 1)

    def prep_rows(self, pool):
        for j in range(MT):
            pool.wait_ge(self.ix, self.same_ready - MT + j + 1)
            self.nc.gpsimd.affine_select(out=self.same[:, j, :], in_=self.same[:, j, :], compare_op=ALU.is_gt, fill=0.0,
                                         base=j * P, pattern=[[-1, NM]], channel_multiplier=1).then_inc(self.keep, 1)

    def prep_bank(self, k):
        return (self.PA[:], self.PX[:, 0:512], self.PX[:, 512:1024])[k % 3]

    def prep_tensor(self, pe):
        mm = self.nc.tensor.matmul
        pe.wait_ge(self.g_w3, 4)
        for k in range((NU + 1) // 2):
            if k >= 3:
                pe.wait_ge(self.p_out, k - 2)
            u = range(2 * k, min(2 * k + 2, NU))
            for j, n in enumerate(u):
                last = mm(self.prep_bank(k)[:, j * D:(j + 1) * D], self.cst[:, C_CTR:C_CTR + P], self.w3g[:, n, :], start=True, stop=True)
            last.then_inc(self.p_mm, 1)
        pe.wait_ge(self.p_out, 3)
        o = self.PX[0:NU, 512:512 + D]
        for n in range(NU):
            mm(o, self.lnb_diag[:, n, :], self.w3[:, n, :], start=n == 0, stop=False)
        mm(o, self.ident[0:NU, 0:NU], self.b3[:], start=False, stop=True).then_inc(self.p_mm, 1)

    def prep_scalar(self, act):
        K = (NU + 1) // 2
        for k in range(K):
            act.wait_ge(self.p_mm, k + 1)
            u = min(2, NU - 2 * k)
            self.nc.scalar.activation(self.w3c[:, 2 * k:2 * k + u, :].rearrange("p u d -> p (u d)"),
                                      self.prep_bank(k)[:, 0:u * D], ACT.Copy).then_inc(self.p_out, 1)
        act.wait_ge(self.p_mm, K + 1)
        self.nc.scalar.activation(self.c3[:], self.PX[0:NU, 512:512 + D], ACT.Copy).then_inc(self.p_out, 1)

    def prep_vector(self, dve):
        v = self.nc.vector
        done = 0

        def link(ins):
            nonlocal done
            done += 1
            ins.then_inc(self.ix, 1)
            dve.wait_ge(self.ix, done)

        dve.wait_ge(self.ix_loaded, 32)
        link(v.tensor_copy(self.idx_f[:], self.idx[:]))
        for k, size in enumerate((B, T)):
            f, w, n, c, ok = (x[:, k, :] for x in (self.idx_f, self.idx_w, self.idx_n, self.idx_c, self.idx_ok))
            link(v.tensor_scalar(w, f, 0.0, float(size), ALU.is_lt, ALU.mult))
            link(v.tensor_tensor(n, f, w, ALU.add))
            link(v.tensor_scalar(c, n, 0.0, float(size - 1), ALU.max, ALU.min))
            link(v.tensor_tensor(ok, c, n, ALU.is_equal))
        link(v.scalar_tensor_tensor(out=self.row_no[:], in0=self.idx_c[:, 0, :], scalar=float(T), in1=self.idx_c[:, 1, :],
                                    op0=ALU.mult, op1=ALU.add))
        link(v.tensor_tensor(self.row_ok[:], self.idx_ok[:, 0, :], self.idx_ok[:, 1, :], ALU.mult))
        link(v.tensor_scalar(self.row_ok[:], self.row_ok[:], -FAR, FAR, ALU.mult, ALU.add))
        link(v.tensor_tensor(self.row_to[:], self.row_no[:], self.row_ok[:], ALU.add))
        link(v.tensor_copy(self.src_row[:], self.row_no[:, 0:MT]))
        assert done == self.gather_ready
        for j in range(MT):
            link(v.tensor_scalar(self.same[:, j, :], self.row_to[:, MT:], self.row_to[:, j:j + 1], 1.0, ALU.is_equal, ALU.mult))
        assert done == self.same_ready
        for j in range(MT):
            dve.wait_ge(self.keep, j + 1)
            link(v.tensor_reduce(self.dup[:, j:j + 1], self.same[:, j, :], AX_X, ALU.max))
        link(v.scalar_tensor_tensor(out=self.to_f[:], in0=self.dup[:], scalar=FAR, in1=self.row_to[:, 0:MT], op0=ALU.mult, op1=ALU.add))
        link(v.tensor_copy(self.dst_row[:], self.to_f[:]))
        assert done == self.scatter_ready


    def gpsimd(self, pool):
        gp = self.nc.gpsimd
        pool.wait_ge(self.x2_stored, 16 * B)
        pool.wait_ge(self.ix, self.gather_ready)
        for j in range(MT):
            gp.indirect_dma_start(out=self.xg[:, j, :], out_offset=None, in_=self.x2_dram,
                                  in_offset=bass.IndirectOffsetOnAxis(ap=self.src_row[:, j:j + 1], axis=0),
                                  bounds_check=B * T - 1, oob_is_err=False).then_inc(self.gather, 16)
        pool.wait_ge(self.gate, self.gate_ready)

        def unit(n, k):
            after_plainly(pool, self.zeroed, (self.mv_s, MT, n, MT), (self.al_s, 1, n - 1, 1))
            gp.tensor_scalar(self.rs[:], self.mv[:, :, 1], 4 * EPS_LN, 1.0, ALU.add, ALU.mult).then_inc(self.rs_s, 1)
            after(pool, self.rs_s, 2, n, 1)
            gp.tensor_tensor(self.rs[:], self.rs[:], self.minus_half[:], ALU.pow).then_inc(self.rs_s, 1)
            after(pool, self.rs_s, 2, n, 2)
            after(pool, self.acc_s, MT, n - 2, MT)
            gp.tensor_tensor(self.alpha[k][:], self.rs[:], self.ow[:, :, n:n + 1].rearrange("p t n -> p (t n)")
                             if isinstance(n, int) else self.ow[:, :, bass.ds(n, 1)].rearrange("p t n -> p (t n)"),
                             ALU.mult).then_inc(self.al_s, 1)

        self.units(pool, unit)
        pool.wait_ge(self.mv4_s, MT)
        gp.tensor_scalar(self.rs4[:], self.mv4[:, :, 1], EPS_LN, 1.0, ALU.add, ALU.mult).then_inc(self.rs4_s, 1)
        pool.wait_ge(self.rs4_s, 1)
        gp.tensor_tensor(self.rs4[:], self.rs4[:], self.minus_half[:], ALU.pow).then_inc(self.rs4_s, 1)
        pool.wait_ge(self.out_stored, 16 * B)
        pool.wait_ge(self.ix, self.scatter_ready)
        rows_out = self.out.rearrange("b t d -> (b t) d")
        for j in range(MT):
            pool.wait_ge(self.yo_s, j + 1)
            gp.indirect_dma_start(out=rows_out, out_offset=bass.IndirectOffsetOnAxis(ap=self.dst_row[:, j:j + 1], axis=0),
                                  in_=self.yo[:, j, :], in_offset=None,
                                  bounds_check=B * T - 1, oob_is_err=False).then_inc(self.scatter, 16)
        pool.wait_ge(self.scatter, 16 * MT)

    def out_bank(self, t):
        return (self.PA, self.PB)[t // 2][:, (t % 2) * D:(t % 2 + 1) * D]

    def tensor(self, pe):
        mm, tr = self.nc.tensor.matmul, self.nc.tensor.transpose
        H_ = (self.PX, self.PS)
        pe.wait_ge(self.gather, 16 * MT)
        pe.wait_ge(self.p_out, (NU + 1) // 2 + 1)
        for t in range(MT):
            for c in range(DC):
                last = tr(self.PX[:, c * NM + t * P:c * NM + (t + 1) * P], self.xg[:, t, c * P:(c + 1) * P], self.ident)
        last.then_inc(self.xgT_mm, 1)
        pe.wait_ge(self.xgT_out, 1)
        for t in range(MT):
            o = self.PC[:, t * NU:(t + 1) * NU]
            for c in range(DC):
                mm(o, self.xgT[:, c, t * P:(t + 1) * P], self.gate_w[:, c, :], start=c == 0, stop=False)
            last = mm(o, self.ones[0:1, :], self.gate_b[:], start=False, stop=True)
        last.then_inc(self.lg_mm, 1)

        def hidden(n, k):
            pe.wait_ge(self.w12_loaded[k], (n - k) * 8 + 16)
            after(pe, self.h_act, 2, n - 2, 2)
            after(pe, self.z1_s, 1, n - 2, 1)
            for r in range(2):
                for c in range(DC):
                    last = mm(H_[k][:, r * NM:(r + 1) * NM], self.w12[k][:, r, c, :], self.xgT[:, c, :], start=c == 0, stop=c == DC - 1)
            last.then_inc(self.h_mm, 1)

        def unit(n, k):
            if not (isinstance(n, int) and n == NU - 1):
                hidden(n + 1, 1 - k)
            after(pe, self.z_s, 1, n, 1)
            after(pe, self.st_s, MT, n - 1, MT)
            for t in range(MT):
                last = tr(self.PT[:, t * P:(t + 1) * P], self.z[k][:, t * P:(t + 1) * P], self.ident)
            last.then_inc(self.zT_mm, 1)
            after(pe, self.acc_s, MT, n - 1, MT)
            w = self.w3c[:, n, :] if isinstance(n, int) else self.w3c[:, bass.ds(n, 1), :].rearrange("p n d -> p (n d)")
            for t in range(MT):
                last = mm(self.out_bank(t), self.z[k][:, t * P:(t + 1) * P], w, start=True, stop=True)
                if t % 2 == 1:
                    last.then_inc(self.o_mm, 1)

        hidden(0, 0)
        pe.wait_ge(self.gate, self.gate_ready)
        for t in range(MT):
            last = tr(self.PT[0:NU, t * P:(t + 1) * P], self.ow[:, t, :], self.ident)
        last.then_inc(self.owT_mm, 1)
        pe.wait_ge(self.owT_out, 1)
        for t in range(MT):
            last = mm(self.out_bank(t), self.owT[:, t * P:(t + 1) * P], self.c3[:], start=True, stop=True)
        last.then_inc(self.c_mm, 1)
        pe.wait_ge(self.acc_0, 2)
        self.units(pe, unit)

    def scalar(self, act):
        a = self.nc.scalar.activation
        H_ = (self.PX, self.PS)
        act.wait_ge(self.xgT_mm, 1)
        a(self.xgT[:].rearrange("p c m -> p (c m)"), self.PX[:], ACT.Copy).then_inc(self.xgT_out, 1)
        act.wait_ge(self.lg_mm, 1)
        a(self.sg[:].rearrange("p t n -> p (t n)"), self.PC[:, 0:MT * NU], ACT.Tanh, scale=0.5).then_inc(self.lg_sig, 1)

        def unit(n, k):
            col = lambda b: b[:, n:n + 1] if isinstance(n, int) else b[:, bass.ds(n, 1)]
            after(act, self.h_mm, 1, n, 1)
            after(act, self.z_s, 1, n - 2, 1)
            a(self.th[k][:], H_[k][:, 0:NM], ACT.Tanh, bias=col(self.hb1), scale=0.5).then_inc(self.h_act, 1)
            a(self.h2[k][:], H_[k][:, NM:2 * NM], ACT.Identity, bias=col(self.b2)).then_inc(self.h_act, 1)

        def gates():
            act.wait_ge(self.gate, self.diff_ready)
            a(self.tdiff[:], self.diff[:], ACT.Tanh, scale=0.5).then_inc(self.sig2, 1)
            act.wait_ge(self.owT_mm, 1)
            a(self.owT[:], self.PT[0:NU, 0:NM], ACT.Copy).then_inc(self.owT_out, 1)

        gates()
        self.units(act, unit)

    def vector(self, dve):
        v = self.nc.vector
        H_ = (self.PX, self.PS)
        done = 0

        def link(ins):
            nonlocal done
            done += 1
            ins.then_inc(self.gate, 1)
            dve.wait_ge(self.gate, done)

        wide = lambda ap: ap[:].unsqueeze(2).to_broadcast([P, MT, NE])
        per_tile = lambda ap: ap.unsqueeze(1).to_broadcast([P, MT, NE])
        dve.wait_ge(self.lg_sig, 1)
        link(v.tensor_scalar(self.score[:], self.sg[:], 0.5, 0.5, ALU.mult, ALU.add))
        link(v.tensor_tensor(self.sel[:], self.score[:, :, 1:NU], per_tile(self.exp_bias[:]), ALU.add))
        link(v.tensor_reduce(self.top[:], self.sel[:], AX_X, ALU.max))
        link(v.tensor_tensor(self.eq[:], self.sel[:], wide(self.top), ALU.is_equal))
        link(v.tensor_tensor(self.rank[:], self.eq[:], per_tile(self.cst[:, C_REV:C_REV + NE]), ALU.mult))
        link(v.tensor_reduce(self.first[:], self.rank[:], AX_X, ALU.max))
        link(v.tensor_tensor(self.onehot[:], per_tile(self.cst[:, C_REV:C_REV + NE]), wide(self.first), ALU.is_equal))
        link(v.tensor_tensor(self.picked[:], self.onehot[:], self.score[:, :, 1:NU], ALU.mult))
        link(v.tensor_reduce(self.tops[:], self.picked[:], AX_X, ALU.add))
        link(v.tensor_tensor(self.diff[:], self.score[:, :, 0], self.tops[:], ALU.subtract))
        assert done == self.diff_ready
        dve.wait_ge(self.sig2, 1)
        link(v.tensor_scalar(self.ow[:, :, 0], self.tdiff[:], 0.5, 0.5, ALU.mult, ALU.add))
        link(v.tensor_scalar(self.ew[:], self.tdiff[:], -0.5, 0.5, ALU.mult, ALU.add))
        link(v.tensor_tensor(self.ow[:, :, 1:NU], self.onehot[:], wide(self.ew), ALU.mult))
        assert done == self.gate_ready

        def product(n, k):
            b1 = self.b1[:, n:n + 1] if isinstance(n, int) else self.b1[:, bass.ds(n, 1)]
            after(dve, self.h_act, 2, n, 2)
            after(dve, self.z_s, 1, n - 2, 1)
            v.scalar_tensor_tensor(out=self.z1[k][:], in0=H_[k][:, 0:NM], scalar=b1, in1=self.h2[k][:],
                                   op0=ALU.add, op1=ALU.mult).then_inc(self.z1_s, 1)
            after(dve, self.z1_s, 1, n, 1)
            after(dve, self.o_mm, 2, n - 2, 2)
            v.scalar_tensor_tensor(out=self.z[k][:], in0=self.th[k][:], scalar=1.0, in1=self.z1[k][:],
                                   op0=ALU.add, op1=ALU.mult).then_inc(self.z_s, 1)

        def unit(n, k):
            after(dve, self.zT_mm, 1, n, 1)
            after(dve, self.mv_s, MT, n - 1, MT)
            after(dve, self.rs_s, 2, n - 1, 2)
            for t in range(MT):
                v.bn_stats(self.st[:, t, :], self.PT[:, t * P:(t + 1) * P]).then_inc(self.st_s, 1)
            for t in range(MT):
                after_plainly(dve, self.zeroed, (self.st_s, MT, n, t + 1))
                v.bn_aggr(self.mv[:, t, :], self.st[:, t, :]).then_inc(self.mv_s, 1)
            if not (isinstance(n, int) and n == NU - 1):
                product(n + 1, 1 - k)
            after(dve, self.al_s, 1, n, 1)
            for t in range(MT):
                after(dve, self.o_mm, 2, n, t // 2 + 1)
                after(dve, self.acc_s, MT, n - 1, t + 1)
                v.scalar_tensor_tensor(out=self.acc[:, t, :], in0=self.out_bank(t), scalar=self.alpha[k][:, t:t + 1],
                                       in1=self.acc[:, t, :], op0=ALU.mult, op1=ALU.add).then_inc(self.acc_s, 1)

        product(0, 0)
        dve.wait_ge(self.c_mm, 1)
        for k, bank in enumerate((self.PA, self.PB)):
            v.tensor_tensor(self.acc[:, 2 * k:2 * k + 2, :].rearrange("p t d -> p (t d)"), bank[:],
                            self.xg[:, 2 * k:2 * k + 2, :].rearrange("p t d -> p (t d)"), ALU.add).then_inc(self.acc_0, 1)
        dve.wait_ge(self.acc_0, 2)
        self.units(dve, unit)
        dve.wait_ge(self.acc_s, MT * NU)
        for t in range(MT):
            v.bn_stats(self.st4[:, t, :], self.acc[:, t, :]).then_inc(self.st4_s, 1)
        for t in range(MT):
            dve.wait_ge(self.st4_s, t + 1)
            v.bn_aggr(self.mv4[:, t, :], self.st4[:, t, :]).then_inc(self.mv4_s, 1)
        dve.wait_ge(self.rs4_s, 2)
        for t in range(MT):
            v.tensor_scalar(self.yo[:, t, :], self.acc[:, t, :], self.mv4[:, t, 0:1], self.rs4[:, t:t + 1],
                            ALU.subtract, ALU.mult).then_inc(self.yo_s, 1)


def constants():
    f = np.float32
    c = np.zeros((P, C_END), f)
    c[:, C_ID:C_ID + P] = np.eye(P)
    c[:, C_CTR:C_CTR + P] = np.eye(P) - 1.0 / FH
    inv = (1.0 / f(10000.0) ** (np.arange(0, DK, 2, dtype=f) / f(DK))).astype(f)

    def angles(n):
        t = (f(10.0) * (np.arange(n, dtype=f) / f(n))).astype(f)
        return np.outer(t, inv).astype(f)

    aq, ak = angles(T), angles(LK)
    cq = np.concatenate([np.cos(aq), np.cos(aq)], 1)
    sq = np.concatenate([-np.sin(aq), np.sin(aq)], 1)
    for t in range(TT):
        c[:, C_COSQ + t * D:C_COSQ + (t + 1) * D] = np.tile(cq[t * P:(t + 1) * P], (1, H))
        c[:, C_SINQ + t * D:C_SINQ + (t + 1) * D] = np.tile(sq[t * P:(t + 1) * P], (1, H))
    c[:, C_COST:C_COST + T] = np.tile(cq.T, (HC, 1))
    c[:, C_SINT:C_SINT + T] = np.tile(sq.T, (HC, 1))
    c[:, C_COSK:C_COSK + LK] = np.tile(np.concatenate([np.cos(ak), np.cos(ak)], 1).T, (HC, 1))
    c[:, C_SINK:C_SINK + LK] = np.tile(np.concatenate([-np.sin(ak), np.sin(ak)], 1).T, (HC, 1))
    p = np.arange(P)
    for j in range(4):
        c[:, C_MASK + j] = (p // DK) % 4 == j
    for j in range(HC):
        c[:, C_HALF + j] = 0.5 * (p // DK == j)
    c[:, C_REV:C_REV + NE] = NE - np.arange(NE)
    return c


def kernel(**inputs):
    import concourse.bacc as bacc
    from concourse.bass_utils import run_bass_kernel_spmd

    i = {k: np.asarray(v) for k, v in inputs.items()}
    a = lambda n: i["L0_attn_" + n]
    x = lambda n: i["L0_xattn_" + n]
    f = lambda n: i["L0_ffn_" + n]
    rot = np.arange(D).reshape(H, 2, DK // 2)[:, ::-1].reshape(-1)

    def by_chunk(m):
        return np.ascontiguousarray(m.reshape(DC, P, -1).transpose(1, 0, 2))

    def vec(v):
        return v.reshape(DC, P).T

    def units(shared, experts):
        return np.concatenate([shared[None], experts])

    arrays = {
        "x": i["x"],
        "xT": np.ascontiguousarray(i["x"].transpose(0, 2, 1).reshape(B, DC, P, T).transpose(0, 2, 1, 3)),
        "ctxT": by_chunk(i["ctx_1024"].transpose(2, 0, 1).reshape(D, CT)),
        "w_aq": by_chunk(a("Wq").T), "w_ak": by_chunk(a("Wk").T), "w_av": by_chunk(a("Wv").T), "w_ao": by_chunk(a("Wo").T),
        "w_xq": by_chunk(x("Wq").T), "w_xk": by_chunk(x("Wk").T), "w_xkr": by_chunk(x("Wk")[rot].T),
        "w_xv": by_chunk(x("Wv").T), "w_xo": by_chunk(x("Wo").T),
        "w_s12": by_chunk(np.concatenate([f("sw1"), f("sw2")]).T), "w3s": np.ascontiguousarray(f("sw3").T),
        "proj": np.ascontiguousarray(a("proj").reshape(DC, HC, M, DK).transpose(1, 3, 0, 2)),
        "bo_a": a("bo").reshape(1, D),
        "rows": np.concatenate([x("bo"), f("sb3"), f("sb3")]).reshape(1, 3, D),
        "cols": np.ascontiguousarray(np.concatenate(
            [vec(x("bq")), vec(x("bq")[rot]), vec(x("bk")), vec(x("bk")[rot]), vec(x("bv")),
             f("sb1")[:, None], f("sb2")[:, None], f("s_ln_g")[:, None], f("s_ln_b")[:, None],
             ], 1)),
        "cst": constants(),
        "w12_units": np.ascontiguousarray(units(np.stack([f("sw1"), f("sw2")]), np.stack([f("ew1"), f("ew2")], 1))
                                          .reshape(NU, 2, FH, DC, P).transpose(0, 4, 1, 3, 2)),
        "w3_units": np.ascontiguousarray(units(f("sw3"), f("ew3")).transpose(2, 0, 1)),
        "b1_units": units(f("sb1"), f("eb1")).T.copy(), "b2_units": units(f("sb2"), f("eb2")).T.copy(),
        "lng_units": units(f("s_ln_g"), np.tile(f("sel_ln_g"), (NE, 1))).T.copy(),
        "lnb_units": units(f("s_ln_b"), np.tile(f("sel_ln_b"), (NE, 1))).T.copy(),
        "b3_units": units(f("sb3"), f("eb3")),
        "gate_w": by_chunk(np.concatenate([f("sg_w"), f("eg_w")]).T),
        "gate_b": np.concatenate([f("sg_b"), f("eg_b")]).reshape(1, NU),
        "exp_bias": f("exp_bias").reshape(1, NE),
        "idx_cols": np.ascontiguousarray(np.stack([f("index_b").reshape(MT, P).T, f("index_t").reshape(MT, P).T], 1)),
        "idx_rows": np.stack([f("index_b"), f("index_t")])[None],
    }
    nc = bacc.Bacc("TRN2", target_bir_lowering=False, num_devices=1)
    g = {n: nc.dram_tensor("in_" + n, v.shape, mybir.dt.from_np(v.dtype), kind="ExternalInput").ap() for n, v in arrays.items()}
    out = nc.dram_tensor("out_0", (B, T, D), F32, kind="ExternalOutput").ap()
    decoder_layer(nc, g, out)
    r = run_bass_kernel_spmd(nc, [{"in_" + n: v for n, v in arrays.items()}], core_ids=[0])
    return r.results[0]["out_0"]
```

```python
from contextlib import ExitStack

import numpy as np

import concourse.bass as bass
from concourse import mybir

ALU = mybir.AluOpType
ACT = mybir.ActivationFunctionType
F32 = mybir.dt.float32
I32 = mybir.dt.int32
U32 = mybir.dt.uint32
AX_X = mybir.AxisListType.X

P = 128
B, T, D = 8, 256, 256
TT = T // P
DC = D // P
H, M, DK = 16, 64, 16
DV = DK + 1
HC = H // DC
PAIRS = H // 2
LK = 77
CT = B * LK
NE, FH, NM = 8, 128, 512
NU = 1 + NE
MT = NM // P
EPS_PHI = 1e-6
EPS_LN = 1e-5
SCALE = DK ** -0.5
FAR = 4096.0

C_ID, C_CTR, C_MASK, C_BLOCK = 0, P, 2 * P, 2 * P + 4
C_HALF = C_BLOCK + HC
C_REV = C_HALF + HC
C_COSK = C_REV + NE
C_SINK = C_COSK + LK
C_COST = C_SINK + LK
C_SINT = C_COST + T
C_COSQ = C_SINT + T
C_SINQ = C_COSQ + TT * D
C_END = C_SINQ + TT * D


def after(eng, sem, per, b, k):
    if isinstance(b, int) and b < 0:
        return
    eng.wait_ge(sem, b * per + k)


def after_plainly(eng, zeroed, *events):
    targets = [(s, b * per + k if isinstance(b, int) else eng.compute_val(b * per + k)) for s, per, b, k in events
               if not (isinstance(b, int) and b < 0)]
    eng.wait_ge(zeroed, 4)
    for s, value in targets:
        eng.wait_ge(s, value)


def decoder_layer(nc, g, out):
    ctx = ExitStack()
    with ctx:
        def sb(name, shape, dt=F32):
            return ctx.enter_context(nc.sbuf_tensor(name, shape, dt))

        def pb(name, cols):
            return ctx.enter_context(nc.psum_tensor(name, [P, cols], F32))

        def sem(name):
            return ctx.enter_context(nc.semaphore(name))

        x2_dram = nc.dram_tensor("x2_rows", [B * T, D], F32, kind="Internal").ap()

        PX = pb("psum_features", 1024)
        PA = pb("psum_a", 512)
        PS = pb("psum_scores", 1024)
        PT = pb("psum_probs_t", 512)
        PB = pb("psum_b", 512)
        PC = pb("psum_c", 512)

        cst = sb("cst", [P, C_END])
        ident = cst[:, C_ID:C_ID + P]
        center = cst[:, C_CTR:C_CTR + P]
        cosq = cst[:, C_COSQ:C_COSQ + TT * D]
        sinq = cst[:, C_SINQ:C_SINQ + TT * D]
        cosT = cst[:, C_COST:C_COST + T]
        sinT = cst[:, C_SINT:C_SINT + T]
        cosk = cst[:, C_COSK:C_COSK + LK]
        sink = cst[:, C_SINK:C_SINK + LK]
        head_mask = cst[:, C_MASK:C_MASK + 4]
        blocks = cst[:, C_BLOCK:C_BLOCK + HC]
        half_blocks = cst[:, C_HALF:C_HALF + HC]
        names = ("aq", "ak", "av", "ao", "xk", "xkr", "xv", "xq", "xo", "s12")
        weights = sb("weights", [P, len(names), DC, D])
        w = {n: weights[:, j] for j, n in enumerate(names)}
        w3s = sb("w3s", [P, D])
        proj = sb("proj", [P, DC, M])
        projbd = sb("projbd", [P, DC, HC * M])
        ctxT = sb("ctxT", [P, DC, CT])
        cols = sb("cols", [P, 14])
        BQ, BQR, BK, BKR, BV, SB1, SB2, SG, SLB = 0, 2, 4, 6, 8, 10, 11, 12, 13
        rows = sb("rows", [1, 3, D])
        bo_a = sb("bo_a", [P, D])
        bo_b = sb("bo_b", [P, D])
        c3_s = sb("c3_s", [P, D])
        w3c_s = sb("w3c_s", [P, D])
        w3g = sb("w3g", [P, D])
        ones = sb("ones", [P, P])
        minus_half = sb("minus_half", [P, MT])
        rbqT = sb("rbqT", [P, DC, T])
        ktr = sb("ktr", [P, DC, CT])
        ktt = sb("ktt", [P, 2, 2, CT // 2])
        vx = sb("vx", [LK, B, H, DV])
        rq_tmp = sb("rq_tmp", [P, DC, T])

        xT = sb("xT", [P, DC, T])
        xrow = sb("xrow", [P, TT, D])
        xb = sb("xb", [P, TT, D])
        qk = sb("qk", [P, 2, DC, T])
        sq = sb("sq", [P, 2, DC, T])
        halfn = sb("halfn", [P, 2, TT, H])
        va = sb("va", [P, TT, H, DV])
        phi = sb("phi", [P, 2, TT, H * M])
        fmax = sb("fmax", [P, 4, H])
        shift = sb("shift", [P, 4, H])
        kvbd = sb("kvbd", [P, PAIRS, 2 * DV])
        phiqT = sb("phiqT", [P, TT, PAIRS, P])
        dena = sb("dena", [P, TT, 2, H])
        oa = sb("oa", [P, TT, D])
        oaT = sb("oaT", [P, TT, DC, P])
        y1 = sb("y1", [P, TT, D])
        st1 = sb("st1", [P, TT, 6])
        mv1 = sb("mv1", [P, TT, 2])
        rs1 = sb("rs1", [P, TT])
        x1 = sb("x1", [P, TT, D])
        x1T = sb("x1T", [P, TT, DC, P])
        x1b = sb("x1b", [P, TT, D])
        qc = sb("qc", [P, TT * D])
        qs = sb("qs", [P, TT * D])
        qr = sb("qr", [P, TT * D])
        qT = sb("qT", [P, DC, T])
        ktbd = sb("ktbd", [P, DC, 4, LK])
        vcur = sb("vcur", [LK, H, DV])
        smax = sb("smax", [P, 4, 8])
        pr = sb("pr", [P, 4, 8 * LK])
        prT = sb("prT", [LK, 2, 4, P])
        denb = sb("denb", [P, TT, H])
        ob = sb("ob", [P, TT, D])
        obT = sb("obT", [P, TT, DC, P])
        y2 = sb("y2", [P, TT, D])
        st2 = sb("st2", [P, TT, 6])
        mv2 = sb("mv2", [P, TT, 2])
        rs2 = sb("rs2", [P, TT])
        x2 = sb("x2", [P, 2, TT, D])[:, 0]
        x2T = sb("x2T", [P, TT, DC, P])
        x2c = sb("x2c", [P, TT, D])
        th = sb("th", [P, T])
        h2 = sb("h2", [P, T])
        z1 = sb("z1", [P, T])
        z = sb("z", [P, T])
        stz = sb("stz", [P, TT, 6])
        mvz = sb("mvz", [P, TT, 2])
        rsz = sb("rsz", [P, TT])
        y3 = sb("y3", [P, TT, D])
        st3 = sb("st3", [P, TT, 6])
        mv3 = sb("mv3", [P, TT, 2])
        rs3 = sb("rs3", [P, TT])
        x3 = sb("x3", [P, TT, D])

        L = {n: sem("load_" + n) for n in ("cst", "tables", "qkw", "proj", "va", "oa", "ctx", "kx", "vx", "xq", "xo", "cols", "ffn")}
        xT_loaded, xrow_loaded = sem("xT_loaded"), sem("xrow_loaded")
        zeroed = sem("zeroed")
        projbd_s = sem("projbd_s")
        pre_pe, pre_dve, pre_act, pre_pool = sem("pre_pe"), sem("pre_dve"), sem("pre_act"), sem("pre_pool")
        k_mm, k_out, q_mm, q_out = sem("k_mm"), sem("k_out"), sem("q_mm"), sem("q_out")
        n_mm, n_out, v_mm, v_out = sem("n_mm"), sem("n_out"), sem("v_mm"), sem("v_out")
        f_mm, f_max, f_shift, f_sub, f_exp, f_eps = (sem(n) for n in ("f_mm", "f_max", "f_shift", "f_sub", "f_exp", "f_eps"))
        kv_mm, kv_out = sem("kv_mm"), sem("kv_out")
        ft_mm, ft_out, num_mm, den_a, rec_a, o_a = (sem(n) for n in ("ft_mm", "ft_out", "num_mm", "den_a", "rec_a", "o_a"))
        oaT_mm, oaT_out, wo_mm, y1_sum, xb_done = (sem(n) for n in ("oaT_mm", "oaT_out", "wo_mm", "y1_sum", "xb_done"))
        st1_s, mv1_s, rs1_s, x1_s = (sem(n) for n in ("st1_s", "mv1_s", "rs1_s", "x1_s"))
        x1T_mm, x1T_out, x1b_s, xq_mm, rope_m, rope_s = (sem(n) for n in ("x1T_mm", "x1T_out", "x1b_s", "xq_mm", "rope_m", "rope_s"))
        qT_mm, qT_out, ktbd_s, vcur_s = (sem(n) for n in ("qT_mm", "qT_out", "ktbd_s", "vcur_s"))
        s_mm, s_max, s_sub, s_exp, pt_mm, pt_out, av_mm = (sem(n) for n in ("s_mm", "s_max", "s_sub", "s_exp", "pt_mm", "pt_out", "av_mm"))
        den_b, o_b, obT_mm, obT_out, wx_mm, y2_sum = (sem(n) for n in ("den_b", "o_b", "obT_mm", "obT_out", "wx_mm", "y2_sum"))
        st2_s, mv2_s, rs2_s, x2_s, x2_stored = (sem(n) for n in ("st2_s", "mv2_s", "rs2_s", "x2_s", "x2_stored"))
        x2T_mm, x2T_out, x2c_s, h_mm, h_act, z1_s, z_s = (sem(n) for n in ("x2T_mm", "x2T_out", "x2c_s", "h_mm", "h_act", "z1_s", "z_s"))
        zT_mm, stz_s, mvz_s, rsz_s, c_mm, y3_sum = (sem(n) for n in ("zT_mm", "stz_s", "mvz_s", "rsz_s", "c_mm", "y3_sum"))
        st3_s, mv3_s, rs3_s, x3_s, out_stored = (sem(n) for n in ("st3_s", "mv3_s", "rs3_s", "x3_s", "out_stored"))

        def steps(eng, step):
            step(0, None, None)
            step(1, 0, None)
            step(2, 1, 0)
            with eng.Fori(3, B) as i:
                step(i, i - 1, i - 2)
            step(None, B - 1, B - 2)
            step(None, None, B - 1)

        hb1 = sb("hb1", [P, 1])
        flat = lambda t, letters: t[:].rearrange("p %s -> p (%s)" % (letters, letters))
        spare = {"phi": flat(phi, "w t f"), "phiqT": flat(phiqT, "t q k"), "weights": flat(weights, "n c d"),
                 "ctxT": flat(ctxT, "c k"), "ktt": flat(ktt, "h r k"), "ktr": flat(ktr, "c k"),
                 "pr": flat(pr, "u k"), "sq": flat(sq, "w c t"), "qk": flat(qk, "w c t"),
                 "qc": qc[:], "qs": qs[:], "qr": qr[:], "x2c": flat(x2c, "t d")}
        D_ = stage_d(nc, sb, spare, sem, g, x2_dram, out, (PX, PA, PS, PT, PB, PC), ones, minus_half, cst, rows,
                     x2_stored, out_stored, zeroed, y1_sum, y3_sum, ft_out)

        block = ctx.enter_context(nc.Block())

        @block.sync
        def _(sp):
            def load_rows(b):
                sp.dma_start(xrow[:], g["x"][b].rearrange("(t p) d -> p t d", p=P)).then_inc(xrow_loaded, 16)

            def load_x(b):
                if not (isinstance(b, int) and b == 0):
                    after(sp, v_mm, 1, b - 1, 1)
                    after(sp, xb_done, 1, b - 1, 1)
                sp.dma_start(xT[:], g["xT"][b]).then_inc(xT_loaded, 16)
                if not (isinstance(b, int) and b == 0):
                    load_rows(b)

            sp.dma_start(w["ak"], g["w_ak"]).then_inc(L["qkw"], 16)
            load_x(0)
            sp.dma_start(w["aq"], g["w_aq"]).then_inc(L["qkw"], 16)
            D_.index_loads(sp)
            sp.dma_start(w["av"], g["w_av"]).then_inc(L["va"], 16)
            load_rows(0)
            sp.dma_start(ctxT[:], g["ctxT"]).then_inc(L["ctx"], 16)
            sp.dma_start(w["xk"], g["w_xk"]).then_inc(L["kx"], 16)
            sp.dma_start(w["xkr"], g["w_xkr"]).then_inc(L["kx"], 16)
            sp.dma_start(w["ao"], g["w_ao"]).then_inc(L["oa"], 16)
            sp.dma_start(bo_a[:], g["bo_a"].to_broadcast([P, D])).then_inc(L["oa"], 16)
            sp.dma_start(w["xv"], g["w_xv"]).then_inc(L["vx"], 16)
            sp.dma_start(w["xq"], g["w_xq"]).then_inc(L["xq"], 16)
            sp.dma_start(w["xo"], g["w_xo"]).then_inc(L["xo"], 16)
            sp.dma_start(w["s12"], g["w_s12"]).then_inc(L["ffn"], 16)
            sp.dma_start(w3s[:], g["w3s"]).then_inc(L["ffn"], 16)
            D_.loads(sp)

            def step(a, b, c):
                if a is not None and not (isinstance(a, int) and a == B - 1):
                    load_x(a + 1)
                if c is not None:
                    after(sp, x3_s, TT, c, TT)
                    sp.dma_start(out[c].rearrange("(t p) d -> p t d", p=P), x3[:]).then_inc(out_stored, 16)
                if b is not None:
                    after(sp, x2_s, TT, b, TT)
                    sp.dma_start(x2_dram.rearrange("(b t p) d -> b p t d", b=B, p=P)[b], x2[:]).then_inc(x2_stored, 16)

            step(0, None, None)
            step(1, 0, None)
            step(2, 1, 0)
            with sp.Fori(3, B - 1) as i:
                step(i, i - 1, i - 2)
            step(B - 1, B - 2, B - 3)
            step(None, B - 1, B - 2)
            step(None, None, B - 1)
            D_.more_loads(sp)
            sp.wait_ge(x2_stored, 16 * B)
            sp.wait_ge(out_stored, 16 * B)

        VALUE_EVENTS = 1 + B // 2

        def values_bank(b):
            half = (b - 1) % 2
            return PT[0:LK, 0:D] if b == 0 else PC[0:LK, half * D:(half + 1) * D]

        @block.tensor
        def _(pe):
            def mm(o, l, r, start=True, stop=True):
                return nc.tensor.matmul(o, l, r, start=start, stop=stop)

            def project(o, lhs, rhs, n):
                for c in range(n):
                    last = mm(o, lhs(c), rhs(c), c == 0, c == n - 1)
                return last

            def pre_keys(c, hb):
                n = CT // 2
                i = 2 * c + hb
                banks = ((PS[:, 0:512], PS[:, 512:1024]), (PT[:], PB[:]))[hb]
                if i == 0:
                    pe.wait_ge(L["ctx"], 16)
                    pe.wait_ge(L["kx"], 32)
                if c == 1:
                    pe.wait_ge(pre_dve, 2 * hb + 2 + 2)
                for r, name in enumerate(("xk", "xkr")):
                    last = project(banks[r][:, 0:n], lambda d: w[name][:, d, c * P:(c + 1) * P],
                                   lambda d: ctxT[:, d, hb * n:(hb + 1) * n], DC)
                last.then_inc(pre_pe, 1)

            def pre_values(b):
                if b == 0:
                    pe.wait_ge(L["vx"], 16)
                    pe.wait_ge(pre_dve, 2 + 8)
                elif b == 1:
                    pe.wait_ge(pre_dve, 13)
                elif b % 2:
                    pe.wait_ge(pre_act, 1 + b // 2)
                if b == 5:
                    pe.wait_ge(n_out, 2)
                project(values_bank(b), lambda d: ctxT[:, d, b * LK:(b + 1) * LK],
                        lambda d: w["xv"][:, d, :], DC).then_inc(pre_pe, 1)

            def pre_bias():
                pe.wait_ge(n_out, 1)
                pe.wait_ge(L["xo"], 16)
                for c in range(DC):
                    mm(PB[:, 0:D], cols[:, BV + c:BV + c + 1].to_broadcast([P, P]), w["xo"][:, c, :], c == 0, False)
                mm(PB[:, 0:D], ones[0:1, :], rows[:, 0, :], False, True).then_inc(pre_pe, 1)
                pe.wait_ge(L["ffn"], 32)
                mm(PB[:, D:2 * D], cols[:, SLB:SLB + 1].to_broadcast([P, P]), w3s[:], True, False)
                mm(PB[:, D:2 * D], ones[0:1, :], rows[:, 1, :], False, True).then_inc(pre_pe, 1)
                pe.wait_ge(pre_pool, 5)
                mm(PC[:, 0:D], center, w3g[:]).then_inc(pre_pe, 1)

            def kq_proj(b, which, weights, done):
                if which == 0:
                    after(pe, xT_loaded, 16, b, 16)
                    after(pe, ft_out, 2, b - 1, 2)
                for c in range(DC):
                    last = project(PX[:, 512 * which + c * T:512 * which + (c + 1) * T], lambda d: weights[:, d, c * P:(c + 1) * P],
                                   lambda d: xT[:, d, :], DC)
                last.then_inc(done, 1)

            def norms(b):
                after(pe, y3_sum, TT, b - 3, TT)
                for which in range(2):
                    for t in range(TT):
                        for c in range(DC):
                            o = ((which * TT + t) * DC + c) * HC
                            last = mm(PC[:, o:o + HC], sq[:, which, c, t * P:(t + 1) * P], half_blocks)
                last.then_inc(n_mm, 1)

            def features(b, u):
                if u > 0:
                    after(pe, f_sub, 4, b, u)
                else:
                    after(pe, q_out, 2, b, 2)
                for c in range(DC):
                    last = mm(PX[:, c * 512:(c + 1) * 512], qk[:, u // 2, c, (u % 2) * P:(u % 2 + 1) * P], projbd[:, c, :])
                last.then_inc(f_mm, 1)

            def values(b):
                after(pe, y1_sum, 1, b - 1, 1)
                for t in range(TT):
                    last = project(PA[:, t * D:(t + 1) * D], lambda d: xT[:, d, t * P:(t + 1) * P],
                                   lambda d: w["av"][:, d, :], DC)
                last.then_inc(v_mm, 1)

            def kv(b, part):
                if part == 0:
                    after(pe, v_out, 1, b, 1)
                    after(pe, f_eps, 2, b, 2)
                for p in range(part * PAIRS // 4, (part + 1) * PAIRS // 4):
                    for t in range(TT):
                        last = mm(PA[:, p * 2 * DV:(p + 1) * 2 * DV], phi[:, 0, t, p * P:(p + 1) * P],
                                  va[:, t, 2 * p:2 * p + 2, :], t == 0, t == TT - 1)
                if part == 3:
                    last.then_inc(kv_mm, 1)

            def features_T(b, t):
                after(pe, f_exp, 4, b, 3 + t)
                if t == 0:
                    after(pe, f_sub, 4, b, 4)
                else:
                    after(pe, ft_out, 2, b, 1)
                for p in range(PAIRS):
                    last = nc.tensor.transpose(PX[:, p * P:(p + 1) * P], phi[:, 1, t, p * P:(p + 1) * P], ident)
                last.then_inc(ft_mm, 1)

            def numerators(b, t):
                after(pe, ft_out, 2, b, t + 1)
                if t == 0:
                    after(pe, kv_out, 2, b, 2)
                else:
                    after(pe, o_a, 2, b, 1)
                for p in range(PAIRS):
                    last = mm(PA[:, p * 2 * DV:(p + 1) * 2 * DV], phiqT[:, t, p, :], kvbd[:, p, :])
                last.then_inc(num_mm, 1)

            def transpose_rows(dst, src):
                for t in range(TT):
                    for c in range(DC):
                        last = nc.tensor.transpose(dst[:, (t * DC + c) * P:(t * DC + c + 1) * P],
                                                   src[:, t, c * P:(c + 1) * P], ident)
                return last

            def rows_times(dst, srcT, weights):
                for t in range(TT):
                    last = project(dst[:, t * D:(t + 1) * D], lambda d: srcT[:, t, d, :], lambda d: weights[:, d, :], DC)
                return last

            def scores(b, u):
                t, c = u // 2, u % 2
                if u == 0:
                    after(pe, qT_out, 1, b, 1)
                    after(pe, ktbd_s, 1, b, 1)
                    after(pe, s_sub, 4, b - 1, 4)
                else:
                    after(pe, s_sub, 4, b, u)
                for s in range(2):
                    last = mm(PS[:, 512 * s:512 * s + 4 * LK], qT[64 * s:64 * s + 64, c, t * P:(t + 1) * P],
                              ktbd[64 * s:64 * s + 64, c, :, :])
                last.then_inc(s_mm, 1)

            def probs_T(b, u, s):
                n = 2 * u + s
                if s == 0:
                    after(pe, s_exp, 4, b, u + 1)
                if n == 0:
                    after(pe, pt_out, 8, b - 1, 8)
                else:
                    after(pe, pt_out, 8, b, n)
                for j in range(4):
                    k = 4 * s + j
                    last = nc.tensor.transpose(PT[0:LK, j * P:(j + 1) * P], pr[:, u, k * LK:(k + 1) * LK], ident)
                last.then_inc(pt_mm, 1)

            def weigh_values(b, u, s):
                n = 2 * u + s
                after(pe, pt_out, 8, b, n + 1)
                if n == 0:
                    after(pe, vcur_s, 1, b, 1)
                    after(pe, qT_out, 1, b, 1)
                if n == 4:
                    after(pe, o_b, 2, b, 1)
                for j in range(4):
                    h = 8 * (u % 2) + 4 * s + j
                    last = mm(PB[:, h * DV:(h + 1) * DV], prT[:, s, j, :], vcur[:, h, :])
                last.then_inc(av_mm, 1)

            def step(a, b, c):
                A, Bb, Cc = a is not None, b is not None, c is not None
                first = isinstance(a, int) and a == 0
                second = isinstance(a, int) and a == 1

                def values_in_step_1(*batches):
                    if isinstance(a, int) and a == 1:
                        for n in batches:
                            pre_values(n)

                values_in_step_1(1, 2)
                if A:
                    if first:
                        pe.wait_ge(L["qkw"], 16)
                    kq_proj(a, 0, w["ak"], k_mm)
                if Bb:
                    numerators(b, 1)
                if A:
                    if first:
                        pe.wait_ge(L["qkw"], 32)
                    kq_proj(a, 1, w["aq"], q_mm)
                if Cc and not A:
                    weigh_values(c, 3, 1)
                if Bb:
                    after(pe, o_a, 2, b, 2)
                    transpose_rows(PA, oa).then_inc(oaT_mm, 1)
                if Cc and A:
                    weigh_values(c, 3, 1)
                values_in_step_1(3, 4)
                if Bb:
                    after(pe, oaT_out, 1, b, 1)
                    if isinstance(b, int) and b == 0:
                        pe.wait_ge(L["oa"], 32)
                    rows_times(PA, oaT, w["ao"]).then_inc(wo_mm, 1)
                if A:
                    if first:
                        pe.wait_ge(projbd_s, DC)
                    features(a, 0)
                if Cc:
                    after(pe, o_b, 2, c, 2)
                    transpose_rows(PB, ob).then_inc(obT_mm, 1)
                if A:
                    if first:
                        pe.wait_ge(L["cst"], 16)
                    if isinstance(a, int) and a == 1:
                        pe.wait_ge(pre_act, 3)
                    if isinstance(a, int) and a == 2:
                        pe.wait_ge(pre_act, VALUE_EVENTS)
                    norms(a)
                elif Bb:
                    D_.prep_tensor(pe, 0)
                    D_.prep_tensor(pe, 1)
                if Cc:
                    after(pe, obT_out, 1, c, 1)
                    rows_times(PB, obT, w["xo"]).then_inc(wx_mm, 1)
                    if not Bb:
                        D_.prep_tensor(pe, 7)
                if Bb:
                    after(pe, x1_s, TT, b, TT)
                    after(pe, pt_out, 8, b - 1, 8)
                    if isinstance(b, int) and b == 0:
                        pe.wait_ge(pre_dve, 13)
                    transpose_rows(PT, x1).then_inc(x1T_mm, 1)
                if first:
                    pe.wait_ge(L["va"], 16)
                    values(a)
                    pe.wait_ge(L["cols"], 32)
                    pre_keys(0, 0)
                    pre_keys(0, 1)
                if second:
                    values(a)
                if A:
                    features(a, 1)
                elif Bb:
                    D_.prep_tensor(pe, 2)
                if first:
                    pre_keys(1, 0)
                elif A and not second:
                    values(a)
                def second_rows():
                    after(pe, x2_s, TT, c, TT)
                    if A:
                        after(pe, n_out, 1, a, 1)
                    after(pe, y3_sum, TT, c - 1, TT)
                    transpose_rows(PC, x2).then_inc(x2T_mm, 1)

                if Cc and A:
                    second_rows()
                if Bb:
                    after(pe, x1T_out, 1, b, 1)
                    after(pe, y2_sum, 1, b - 1, 1)
                    if isinstance(b, int) and b == 0:
                        pe.wait_ge(L["xq"], 16)
                    rows_times(PB, x1T, w["xq"]).then_inc(xq_mm, 1)
                if Cc and not A:
                    second_rows()
                if A:
                    features(a, 2)
                    if first:
                        pre_keys(1, 1)
                elif Bb:
                    D_.prep_tensor(pe, 3)
                    D_.prep_tensor(pe, 4)
                if Bb:
                    after(pe, rope_s, 1, b, 1)
                    for t in range(TT):
                        for d in range(DC):
                            last = nc.tensor.transpose(PB[:, d * T + t * P:d * T + (t + 1) * P],
                                                       qr[:, t * D + d * P:t * D + (d + 1) * P], ident)
                    last.then_inc(qT_mm, 1)
                if A:
                    kv(a, 0)
                if Bb:
                    scores(b, 0)
                if Cc:
                    after(pe, x2T_out, 1, c, 1)
                    for r in range(2):
                        last = project(PC[:, r * T:(r + 1) * T], lambda d: w["s12"][:, d, r * FH:(r + 1) * FH],
                                       lambda d: x2T[:, :, d, :], DC)
                    last.then_inc(h_mm, 1)
                values_in_step_1(5, 6)
                if A:
                    kv(a, 1)
                if Bb:
                    probs_T(b, 0, 0)
                    scores(b, 1)
                if A and not first:
                    kv(a, 2)
                if Bb:
                    probs_T(b, 0, 1)
                if A:
                    features(a, 3)
                if first:
                    kv(a, 2)
                if Bb:
                    weigh_values(b, 0, 0)
                if Cc:
                    after(pe, z_s, 1, c, 1)
                    after(pe, h_act, 2, c, 2)
                    for t in range(TT):
                        last = nc.tensor.transpose(PC[:, t * FH:(t + 1) * FH], z[:, t * P:(t + 1) * P], ident)
                    last.then_inc(zT_mm, 1)
                if first:
                    pre_values(0)
                    pre_bias()
                if Bb:
                    weigh_values(b, 0, 1)
                    probs_T(b, 1, 0)
                    scores(b, 2)
                if Bb and not A:
                    D_.prep_tensor(pe, 5)
                if A:
                    kv(a, 3)
                if Bb:
                    probs_T(b, 1, 1)
                    weigh_values(b, 1, 0)
                if A:
                    features_T(a, 0)
                if Bb:
                    weigh_values(b, 1, 1)
                    probs_T(b, 2, 0)
                if Bb:
                    scores(b, 3)
                    probs_T(b, 2, 1)
                    weigh_values(b, 2, 0)
                values_in_step_1(7)
                if Cc:
                    after(pe, stz_s, TT, c, TT)
                    mm(PC[:, 0:D], z[:, 0:P], w3c_s[:])
                if A:
                    numerators(a, 0)
                if Cc:
                    mm(PC[:, D:2 * D], z[:, P:2 * P], w3c_s[:]).then_inc(c_mm, 1)
                if Bb:
                    weigh_values(b, 2, 1)
                    probs_T(b, 3, 0)
                if Bb and not A:
                    D_.prep_tensor(pe, 6)
                if A:
                    features_T(a, 1)
                if Bb:
                    probs_T(b, 3, 1)
                    weigh_values(b, 3, 0)

            steps(pe, step)
            D_.tensor(pe)

        @block.scalar
        def _(act):
            def cp(o, i, s=1.0):
                return nc.scalar.activation(o, i, ACT.Copy, scale=s)

            def out_of(b, mm_s, per, k, o, i, done):
                after(act, mm_s, per, b, k)
                cp(o, i).then_inc(done, 1)

            def kq(b, which, mm_s, done):
                after(act, mm_s, 1, b, 1)
                after(act, f_mm, 4, b - 1, 2 * which + 2)
                after(act, n_mm, 1, b - 1, 1)
                flat = "p c t -> p (c t)"
                bank = PX[:, 512 * which:512 * (which + 1)]
                cp(qk[:, which].rearrange(flat), bank, SCALE).then_inc(done, 1)
                nc.scalar.activation(sq[:, which].rearrange(flat), bank, ACT.Square, scale=SCALE).then_inc(done, 1)

            def f_exponent(b, u):
                after(act, f_sub, 4, b, u + 1)
                f = phi[:, u // 2, u % 2, :]
                nc.scalar.activation(f, f, ACT.Exp).then_inc(f_exp, 1)
                if u < 2:
                    after(act, f_exp, 4, b, u + 1)
                    nc.scalar.activation(f, f, ACT.Copy, bias=EPS_PHI).then_inc(f_eps, 1)

            def s_exponent(b, u):
                after(act, s_sub, 4, b, u + 1)
                nc.scalar.activation(pr[:, u, :], pr[:, u, :], ACT.Exp, scale=SCALE).then_inc(s_exp, 1)

            def pt(b, n):
                s = n % 2
                after(act, pt_mm, 8, b, n + 1)
                if n >= 2:
                    after(act, av_mm, 8, b, n - 1)
                else:
                    after(act, av_mm, 8, b - 1, 7 + n)
                cp(prT[:, s].rearrange("k j t -> k (j t)"), PT[0:LK, :]).then_inc(pt_out, 1)

            def ft(b, t):
                after(act, ft_mm, 2, b, t + 1)
                after(act, num_mm, 2, b - 1, t + 1)
                nc.scalar.activation(phiqT[:, t].rearrange("p q t -> p (q t)"), PX[:], ACT.Copy,
                                     bias=EPS_PHI).then_inc(ft_out, 1)

            def pre_value(*batches):
                b, n = batches[0], len(batches)
                if b == 0:
                    act.wait_ge(zeroed, 4)
                act.wait_ge(pre_pe, 8 + batches[-1] if b else 4 + 1)
                cp(vx[:, b:b + n, :, 0:DK], (PC if b else PT)[0:LK, 0:n * D].rearrange("p (b h k) -> p b h k", b=n, k=DK)).then_inc(pre_act, 1)

            def step(a, b, c):
                A, Bb, Cc = a is not None, b is not None, c is not None
                first = isinstance(a, int) and a == 0

                def values_in_step_1(*batches):
                    if isinstance(a, int) and a == 1:
                        pre_value(*batches)

                values_in_step_1(1, 2)
                if A:
                    kq(a, 0, k_mm, k_out)
                    kq(a, 1, q_mm, q_out)
                values_in_step_1(3, 4)
                if Cc:
                    after(act, wx_mm, 1, c - 1, 1)
                    out_of(c, obT_mm, 1, 1, obT[:].rearrange("p t c q -> p (t c q)"), PB[:], obT_out)
                    if not Bb:
                        D_.prep_scalar(act, 5)
                if Bb:
                    after(act, xq_mm, 1, b - 1, 1)
                    out_of(b, x1T_mm, 1, 1, x1T[:].rearrange("p t c q -> p (t c q)"), PT[:], x1T_out)
                if A:
                    after(act, v_mm, 1, a, 1)
                    after(act, kv_mm, 1, a - 1, 1)
                    if first:
                        act.wait_ge(zeroed, 3)
                    cp(va[:, :, :, 0:DK].rearrange("p t h k -> p (t h) k"),
                       PA[:].rearrange("p (g k) -> p g k", k=DK)).then_inc(v_out, 1)
                elif Bb:
                    D_.prep_scalar(act, 0)
                    D_.prep_scalar(act, 1)
                if A:
                    f_exponent(a, 0)
                elif Bb:
                    D_.prep_scalar(act, 2)
                if Cc:
                    after(act, h_mm, 1, c - 1, 1)
                    out_of(c, x2T_mm, 1, 1, x2T[:].rearrange("p t c q -> p (t c q)"), PC[:], x2T_out)
                if A:
                    f_exponent(a, 1)
                elif Bb:
                    D_.prep_scalar(act, 3)
                    D_.prep_scalar(act, 4)
                if Bb:
                    s_exponent(b, 0)
                values_in_step_1(5, 6)
                if Cc:
                    after(act, h_mm, 1, c, 1)
                    after(act, z_s, 1, c - 1, 1)
                    if isinstance(c, int) and c == 0:
                        act.wait_ge(pre_pool, 6)
                    nc.scalar.activation(th[:], PC[:, 0:T], ACT.Tanh, bias=hb1[:], scale=0.5).then_inc(h_act, 1)
                    nc.scalar.activation(h2[:], PC[:, T:2 * T], ACT.Identity, bias=cols[:, SB2:SB2 + 1]).then_inc(h_act, 1)
                if Bb:
                    pt(b, 0)
                if A:
                    f_exponent(a, 2)
                if Bb:
                    pt(b, 1)
                    s_exponent(b, 1)
                if Bb:
                    pt(b, 2)
                if first:
                    pre_value(0)
                if A:
                    f_exponent(a, 3)
                if Bb:
                    pt(b, 3)
                    s_exponent(b, 2)
                if A:
                    ft(a, 0)
                if Bb:
                    pt(b, 4)
                if Bb:
                    pt(b, 5)
                    s_exponent(b, 3)
                values_in_step_1(7)
                if Bb:
                    pt(b, 6)
                if A:
                    ft(a, 1)
                if Bb:
                    pt(b, 7)

            act.dma_start(proj[:], g["proj"]).then_inc(L["proj"], 16)
            act.dma_start(cst[:, 0:C_COSK], g["cst"][:, 0:C_COSK]).then_inc(L["cst"], 16)
            act.dma_start(cols[:], g["cols"]).then_inc(L["cols"], 16)
            act.dma_start(rows[:], g["rows"]).then_inc(L["cols"], 16)
            act.dma_start(cst[:, C_COSK:C_END], g["cst"][:, C_COSK:C_END]).then_inc(L["tables"], 16)
            act.wait_ge(L["cols"], 32)
            steps(act, step)
            D_.scalar(act)


        @block.vector
        def _(dve):
            tt, tsc, stt = nc.vector.tensor_tensor, nc.vector.tensor_scalar, nc.vector.scalar_tensor_tensor

            def f_maximum(b, u):
                after(dve, f_mm, 4, b, u + 1)
                after(dve, f_shift, 4, b - 1, u + 1)
                nc.vector.tensor_reduce(fmax[:, u, :], PX[:].rearrange("p (h m) -> p h m", m=M), AX_X, ALU.max).then_inc(f_max, 1)

            def f_subtract(b, u):
                after(dve, f_max, 4, b, u + 1)
                after(dve, n_out, 1, b, 1)
                after(dve, f_sub, 4, b - 1, u + 1)
                tt(shift[:, u, :], fmax[:, u, :], halfn[:, u // 2, u % 2, :], ALU.add).then_inc(f_shift, 1)
                after(dve, f_shift, 4, b, u + 1)
                if u < 2:
                    after(dve, kv_mm, 1, b - 1, 1)
                else:
                    after(dve, ft_mm, 2, b - 1, u - 1)
                tt(phi[:, u // 2, u % 2, :].rearrange("p (h m) -> p h m", m=M), PX[:].rearrange("p (h m) -> p h m", m=M),
                   shift[:, u, :].unsqueeze(2).to_broadcast([P, H, M]), ALU.subtract).then_inc(f_sub, 1)

            def banks(ap):
                return ap.rearrange("p (s f) -> p s f", s=2)[:, :, 0:4 * LK].rearrange("p s (j k) -> p s j k", k=LK)

            def s_maximum(b, u):
                after(dve, s_mm, 4, b, u + 1)
                after(dve, s_sub, 4, b - 1, u + 1)
                nc.vector.tensor_reduce(smax[:, u, :].rearrange("p (s j) -> p s j", s=2), banks(PS[:]), AX_X, ALU.max).then_inc(s_max, 1)

            def s_subtract(b, u):
                after(dve, s_max, 4, b, u + 1)
                after(dve, pt_mm, 8, b - 1, 2 * u + 2)
                tt(pr[:, u, :].rearrange("p (s j k) -> p s j k", s=2, k=LK), banks(PS[:]),
                   smax[:, u, :].rearrange("p (s j) -> p s j", s=2).unsqueeze(3).to_broadcast([P, 2, 4, LK]),
                   ALU.subtract).then_inc(s_sub, 1)

            def heads(ap):
                return ap[:, 0:H * DV].rearrange("p (h k) -> p h k", k=DV)

            def norm_a(b, t):
                after(dve, num_mm, 2, b, t + 1)
                after(dve, rec_a, 2, b - 1, t + 1)
                tsc(dena[:, t, 0, :], heads(PA[:])[:, :, DK], M * EPS_PHI, None, ALU.add).then_inc(den_a, 1)
                after(dve, den_a, 2, b, t + 1)
                after(dve, o_a, 2, b - 1, t + 1)
                nc.vector.reciprocal(dena[:, t, 1, :], dena[:, t, 0, :]).then_inc(rec_a, 1)
                after(dve, rec_a, 2, b, t + 1)
                after(dve, oaT_mm, 1, b - 1, 1)
                tt(oa[:, t, :].rearrange("p (h k) -> p h k", k=DK), heads(PA[:])[:, :, 0:DK],
                   dena[:, t, 1, :].unsqueeze(2).to_broadcast([P, H, DK]), ALU.mult).then_inc(o_a, 1)

            def norm_b(b, t):
                after(dve, av_mm, 8, b, 4 * t + 4)
                after(dve, o_b, 2, b - 1, t + 1)
                nc.vector.reciprocal(denb[:, t, :], heads(PB[:])[:, :, DK]).then_inc(den_b, 1)
                after(dve, den_b, 2, b, t + 1)
                after(dve, obT_mm, 1, b - 1, 1)
                tt(ob[:, t, :].rearrange("p (h k) -> p h k", k=DK), heads(PB[:])[:, :, 0:DK],
                   denb[:, t, :].unsqueeze(2).to_broadcast([P, H, DK]), ALU.mult).then_inc(o_b, 1)

            def statistics(b, y, st, mv, st_s, mv_s, rs_s):
                after(dve, mv_s, TT, b - 1, TT)
                after(dve, rs_s, 2, b - 1, 2)
                for t in range(TT):
                    nc.vector.bn_stats(st[:, t, :], y(t)).then_inc(st_s, 1)
                for t in range(TT):
                    after_plainly(dve, zeroed, (st_s, TT, b, t + 1))
                    nc.vector.bn_aggr(mv[:, t, :], st[:, t, :]).then_inc(mv_s, 1)

            def normalize(b, y, mv, rs, rs_s, x, x_s):
                after(dve, rs_s, 2, b, 2)
                for t in range(TT):
                    tsc(x[:, t, :], y[:, t, :], mv[:, t, 0:1], rs[:, t:t + 1], ALU.subtract, ALU.mult).then_inc(x_s, 1)

            def pre_queries():
                dve.wait_ge(L["tables"], 16)
                dve.wait_ge(L["cols"], 32)
                for c in range(DC):
                    tsc(rq_tmp[:, c, :], cosT, cols[:, BQ + c:BQ + c + 1], None, ALU.mult).then_inc(pre_dve, 1)
                dve.wait_ge(pre_dve, 2)
                for c in range(DC):
                    stt(out=rbqT[:, c, :], in0=sinT, scalar=cols[:, BQR + c:BQR + c + 1], in1=rq_tmp[:, c, :],
                        op0=ALU.mult, op1=ALU.add)

            def pre_keys(i):
                c, hb = i // 2, i % 2
                n = B // 2
                dve.wait_ge(pre_pe, i + 1)
                if i >= 2:
                    dve.wait_ge(pre_pool, i - 1)
                banks = ((PS[:, 0:512], PS[:, 512:1024]), (PT[:], PB[:]))[hb]
                for r, (bias, table) in enumerate(((BK, cosk), (BKR, sink))):
                    stt(out=ktt[:, hb, r, :].rearrange("p (b k) -> p b k", k=LK),
                        in0=banks[r][:, 0:n * LK].rearrange("p (b k) -> p b k", k=LK),
                        scalar=cols[:, bias + c:bias + c + 1], in1=table.unsqueeze(1).to_broadcast([P, n, LK]),
                        op0=ALU.add, op1=ALU.mult).then_inc(pre_dve, 1)

            def pre_bias():
                dve.wait_ge(pre_pe, 4 + 1 + 2)
                nc.vector.tensor_copy(bo_b[:], PB[:, 0:D]).then_inc(pre_dve, 1)
                nc.vector.tensor_copy(c3_s[:], PB[:, D:2 * D]).then_inc(pre_dve, 1)
                dve.wait_ge(pre_pe, 4 + 1 + 3)
                nc.vector.tensor_copy(w3c_s[:], PC[:, 0:D]).then_inc(pre_dve, 1)

            def step(a, b, c):
                A, Bb, Cc = a is not None, b is not None, c is not None
                first = isinstance(a, int) and a == 0
                if Bb:
                    norm_a(b, 1)
                    after(dve, oaT_mm, 1, b, 1)
                    after(dve, wo_mm, 1, b - 1, 1)
                    nc.vector.tensor_copy(oaT[:].rearrange("p t c q -> p (t c q)"), PA[:]).then_inc(oaT_out, 1)
                if Cc:
                    norm_b(c, 1)
                if Bb:
                    after(dve, wo_mm, 1, b, 1)
                    after(dve, xb_done, 1, b, 1)
                    after(dve, x1_s, TT, b - 1, TT)
                    tt(y1[:].rearrange("p t d -> p (t d)"), PA[:], xb[:].rearrange("p t d -> p (t d)"), ALU.add).then_inc(y1_sum, 1)
                    after(dve, y1_sum, 1, b, 1)
                    statistics(b, lambda t: y1[:, t, :], st1, mv1, st1_s, mv1_s, rs1_s)
                if A:
                    f_maximum(a, 0)
                if Bb:
                    after(dve, x1T_mm, 1, b - 1, 1)
                    after(dve, x1b_s, 1, b - 1, 1)
                    normalize(b, y1, mv1, rs1, rs1_s, x1, x1_s)
                if A:
                    after(dve, n_mm, 1, a, 1)
                    after(dve, f_shift, 4, a - 1, 4)
                    nc.vector.tensor_copy(halfn[:].rearrange("p w t h -> p (w t h)"), PC[:, 0:4 * H]).then_inc(n_out, 1)
                    f_subtract(a, 0)
                if Cc:
                    after(dve, wx_mm, 1, c, 1)
                    after(dve, x1b_s, 1, c, 1)
                    after(dve, x2_s, TT, c - 1, TT)
                    tt(y2[:].rearrange("p t d -> p (t d)"), PB[:], x1b[:].rearrange("p t d -> p (t d)"), ALU.add).then_inc(y2_sum, 1)
                    after(dve, y2_sum, 1, c, 1)
                    statistics(c, lambda t: y2[:, t, :], st2, mv2, st2_s, mv2_s, rs2_s)
                if first:
                    pre_keys(0)
                    pre_keys(1)
                if Cc:
                    after(dve, x2T_mm, 1, c - 1, 1)
                    after(dve, x2c_s, 1, c - 1, 1)
                    after(dve, x2_stored, 16, c - 1, 16)
                    normalize(c, y2, mv2, rs2, rs2_s, x2, x2_s)
                if A:
                    f_maximum(a, 1)
                    f_subtract(a, 1)
                if first:
                    pre_keys(2)
                if Bb:
                    after(dve, xq_mm, 1, b, 1)
                    after(dve, rope_s, 1, b - 1, 1)
                    tt(qc[:], PB[:], cosq, ALU.mult).then_inc(rope_m, 1)
                    view = lambda ap: ap.rearrange("p (g s e) -> p g s e", s=2, e=DK // 2)
                    for s in range(2):
                        tt(view(qs[:])[:, :, s, :], view(PB[:])[:, :, 1 - s, :], view(sinq)[:, :, s, :], ALU.mult).then_inc(rope_m, 1)
                    after(dve, rope_m, 3, b, 3)
                    after(dve, qT_mm, 1, b - 1, 1)
                    tt(qr[:], qc[:], qs[:], ALU.add).then_inc(rope_s, 1)
                if Bb:
                    after(dve, qT_mm, 1, b, 1)
                    after(dve, s_mm, 4, b - 1, 4)
                    tt(qT[:].rearrange("p c t -> p (c t)"), PB[:], rbqT[:].rearrange("p c t -> p (c t)"), ALU.add).then_inc(qT_out, 1)
                if A:
                    f_maximum(a, 2)
                if Bb:
                    s_maximum(b, 0)
                    s_subtract(b, 0)
                if A:
                    f_subtract(a, 2)
                if first:
                    pre_keys(3)
                if Cc:
                    after(dve, h_act, 2, c, 2)
                    after(dve, z_s, 1, c - 1, 1)
                    stt(out=z1[:], in0=PC[:, 0:T], scalar=cols[:, SB1:SB1 + 1], in1=h2[:], op0=ALU.add, op1=ALU.mult).then_inc(z1_s, 1)
                if Bb:
                    s_maximum(b, 1)
                    s_subtract(b, 1)
                if Cc:
                    after(dve, z1_s, 1, c, 1)
                    after(dve, c_mm, 1, c - 1, 1)
                    stt(out=z[:], in0=th[:], scalar=1.0, in1=z1[:], op0=ALU.add, op1=ALU.mult).then_inc(z_s, 1)
                if A:
                    f_maximum(a, 3)
                    f_subtract(a, 3)
                if first:
                    pre_bias()
                    D_.prep_same(dve)
                if Cc:
                    after(dve, zT_mm, 1, c, 1)
                    statistics(c, lambda t: PC[:, t * FH:(t + 1) * FH], stz, mvz, stz_s, mvz_s, rsz_s)
                if Bb:
                    s_maximum(b, 2)
                    s_subtract(b, 2)
                if A:
                    after(dve, kv_mm, 1, a, 1)
                    after(dve, num_mm, 2, a - 1, 2)
                    if first:
                        dve.wait_ge(zeroed, 4)
                    src = PA[:, 0:H * DV].rearrange("p (q k) -> p q k", k=2 * DV)
                    for s in range(2):
                        nc.vector.tensor_copy(kvbd[64 * s:64 * s + 64, :, s * DV:(s + 1) * DV],
                                              src[64 * s:64 * s + 64, :, s * DV:(s + 1) * DV]).then_inc(kv_out, 1)
                if Bb:
                    norm_b(b, 0)
                    s_maximum(b, 3)
                    s_subtract(b, 3)
                if A:
                    norm_a(a, 0)
                if first:
                    D_.prep_targets(dve)
                if Cc:
                    after(dve, c_mm, 1, c, 1)
                    after(dve, rsz_s, 2, c, 2)
                    after(dve, x2c_s, 1, c, 1)
                    after(dve, x3_s, TT, c - 1, TT)
                    for t in range(TT):
                        stt(out=y3[:, t, :], in0=PC[:, t * D:(t + 1) * D], scalar=rsz[:, t:t + 1], in1=x2c[:, t, :],
                            op0=ALU.mult, op1=ALU.add).then_inc(y3_sum, 1)
                    after(dve, y3_sum, TT, c, TT)
                    statistics(c, lambda t: y3[:, t, :], st3, mv3, st3_s, mv3_s, rs3_s)
                if Cc:
                    after(dve, out_stored, 16, c - 1, 16)
                    normalize(c, y3, mv3, rs3, rs3_s, x3, x3_s)

            D_.prep_numbers(dve)
            pre_queries()
            steps(dve, step)
            D_.vector(dve)

        @block.gpsimd
        def _(pool):
            gp = nc.gpsimd

            def rstd(b, mv, mv_s, eps, rs, rs_s, last_use, per):
                after_plainly(pool, zeroed, (mv_s, TT, b, TT), (last_use, per, b - 1, per))
                gp.tensor_scalar(rs[:], mv[:, :, 1], eps, 1.0, ALU.add, ALU.mult).then_inc(rs_s, 1)
                after(pool, rs_s, 2, b, 1)
                gp.tensor_tensor(rs[:], rs[:], minus_half[:, 0:TT], ALU.pow).then_inc(rs_s, 1)

            def add_bias(dst, src, bias, done):
                gp.tensor_tensor(dst[:], src[:], bias[:].unsqueeze(1).to_broadcast([P, TT, D]), ALU.add).then_inc(done, 1)

            def pre_keys(i):
                n, c, hb = CT // 2, i // 2, i % 2
                pool.wait_ge(pre_dve, 2 + 2 * i + 2)
                gp.tensor_tensor(ktr[:, c, hb * n:(hb + 1) * n], ktt[:, hb, 0, :], ktt[:, hb, 1, :], ALU.add).then_inc(pre_pool, 1)

            def pre_ffn():
                pool.wait_ge(L["ffn"], 32)
                gp.tensor_scalar(w3g[:], w3s[:], cols[:, SG:SG + 1], 1.0, ALU.mult, ALU.mult).then_inc(pre_pool, 1)
                gp.tensor_scalar(hb1[:], cols[:, SB1:SB1 + 1], 0.5, 0.0, ALU.mult, ALU.add).then_inc(pre_pool, 1)

            def step(a, b, c):
                A, Bb, Cc = a is not None, b is not None, c is not None
                first = isinstance(a, int) and a == 0
                if Bb and not A:
                    pool.wait_ge(ft_mm, 2 * B)
                    D_.prep_gpsimd(pool)
                if Bb:
                    after(pool, s_mm, 4, b - 1, 4)
                    for c2 in range(DC):
                        ins = gp.tensor_tensor(ktbd[:, c2, :, :],
                                               ktr[:, c2, :].rearrange("p (b k) -> p b k", b=B)[:, bass.ds(b, 1), :].to_broadcast([P, 4, LK]),
                                               head_mask.unsqueeze(2).to_broadcast([P, 4, LK]), ALU.mult)
                    ins.then_inc(ktbd_s, 1)
                    if isinstance(b, int) and b == 1:
                        pool.wait_ge(pre_act, VALUE_EVENTS)
                    after(pool, av_mm, 8, b - 1, 8)
                    gp.tensor_copy(vcur[:].rearrange("k h e -> k (h e)"),
                                   vx[:].rearrange("k b h e -> k b (h e)")[:, bass.ds(b, 1), :].rearrange("k b f -> k (b f)")).then_inc(vcur_s, 1)
                if Bb:
                    rstd(b, mv1, mv1_s, EPS_LN, rs1, rs1_s, x1_s, TT)
                if Cc:
                    rstd(c, mv2, mv2_s, EPS_LN, rs2, rs2_s, x2_s, TT)
                if A:
                    after(pool, xrow_loaded, 16, a, 16)
                    after(pool, y1_sum, 1, a - 1, 1)
                    if first:
                        pool.wait_ge(L["oa"], 32)
                    add_bias(xb, xrow, bo_a, xb_done)
                if first:
                    pre_keys(0)
                    pre_keys(1)
                if Bb:
                    after(pool, x1_s, TT, b, TT)
                    after(pool, y2_sum, 1, b - 1, 1)
                    add_bias(x1b, x1, bo_b, x1b_s)
                if first:
                    pre_keys(2)
                    pre_keys(3)
                if first:
                    pre_ffn()
                    D_.prep_rows(pool)
                    pool.wait_ge(pre_pool, 6)
                    pool.wait_ge(pre_act, 1)
                    pool.wait_ge(pre_dve, 13)
                if Cc:
                    after(pool, x2_s, TT, c, TT)
                    after(pool, y3_sum, TT, c - 1, TT)
                    add_bias(x2c, x2, c3_s, x2c_s)
                if not A and not Bb:
                    D_.gather_rows(pool)
                if Cc:
                    rstd(c, mvz, mvz_s, 4 * EPS_LN, rsz, rsz_s, y3_sum, TT)
                    rstd(c, mv3, mv3_s, EPS_LN, rs3, rs3_s, x3_s, TT)

            gp.memset(ones[:], 1.0).then_inc(zeroed, 1)
            pool.wait_ge(L["proj"], 16)
            pool.wait_ge(L["cst"], 16)
            for c in range(DC):
                gp.tensor_tensor(projbd[:, c, :].rearrange("p (h m) -> p h m", m=M),
                                 proj[:, c, :].unsqueeze(1).to_broadcast([P, HC, M]),
                                 blocks.unsqueeze(2).to_broadcast([P, HC, M]), ALU.mult).then_inc(projbd_s, 1)
            gp.memset(minus_half[:], -0.5).then_inc(zeroed, 1)
            gp.memset(va[:, :, :, DK:DV], 1.0)
            gp.memset(vx[:, :, :, DK:DV], 1.0).then_inc(zeroed, 1)
            gp.memset(kvbd[:], 0.0).then_inc(zeroed, 1)
            steps(pool, step)
            D_.gpsimd(pool)


class stage_d:

    def __init__(self, nc, sb, spare, sem, g, x2_dram, out, banks, ones, minus_half, cst, rows,
                 x2_stored, out_stored, zeroed, y1_sum, y3_sum, ft_out):
        self.nc, self.g, self.x2_dram, self.out = nc, g, x2_dram, out
        self.PX, self.PA, self.PS, self.PT, self.PB, self.PC = banks
        self.ones, self.minus_half, self.cst, self.rows = ones, minus_half, cst, rows
        self.x2_stored, self.out_stored, self.zeroed, self.y1_sum = x2_stored, out_stored, zeroed, y1_sum
        self.y3_sum, self.ft_out = y3_sum, ft_out
        self.ident = cst[:, C_ID:C_ID + P]
        self.w12 = [sb(f"w12_{n}", [P, 2, DC, FH]) for n in range(2)]
        self.w3 = sb("w3_units", [P, NU, D])
        self.w3g = spare["phi"][:, 0:NU * D].rearrange("p (n d) -> p n d", n=NU)
        self.w3c = sb("w3c_units", [P, NU, D])
        self.b1 = sb("b1_units", [P, NU])
        self.hb1 = sb("hb1_units", [P, NU])
        self.b2 = sb("b2_units", [P, NU])
        self.lng = sb("lng_units", [P, NU])
        self.lnb = sb("lnb_units", [P, NU])
        self.lnb_diag = sb("lnb_diag", [P, NU, NU])
        self.b3 = sb("b3_units", [NU, D])
        self.c3 = sb("c3_units", [NU, D])
        self.gate_w = sb("gate_w", [P, DC, NU])
        self.gate_b = sb("gate_b", [P, NU])
        self.exp_bias = sb("exp_bias", [P, NE])
        W = MT + NM
        self.idx = sb("idx_int", [P, 2, W], I32)
        self.idx_f, self.idx_w = (spare["pr"][:, 2 * W * j:2 * W * (j + 1)].rearrange("p (k w) -> p k w", k=2) for j in range(2))
        self.row_to = sb("row_to", [P, W])
        self.same = [spare[name] for name in ("qc", "qs", "qr", "x2c")]
        self.dup = sb("dup", [P, MT])
        self.to_f = sb("to_f", [P, MT])
        self.src_row = sb("src_row", [P, MT], U32)
        self.dst_row = sb("dst_row", [P, MT], U32)
        rows_of = lambda name, at: spare[name][:, at:at + MT * D].rearrange("p (t d) -> p t d", t=MT)
        self.xg, self.acc, self.yo = rows_of("pr", 0), rows_of("pr", MT * D), rows_of("qk", 0)
        self.xgT = spare["sq"].rearrange("p (c m) -> p c m", c=DC)
        wide = lambda j: spare["phi"][:, j * NM:(j + 1) * NM]
        self.z1, self.z, self.th, self.h2 = ([wide(2 * j), wide(2 * j + 1)] for j in range(4))
        self.st = sb("st_d", [P, MT, 6])
        self.mv = sb("mv_d", [P, MT, 2])
        self.rs = sb("rs_d", [P, MT])
        self.alpha = [sb(f"alpha_d{n}", [P, MT]) for n in range(2)]
        self.st4 = sb("st4", [P, MT, 6])
        self.mv4 = sb("mv4", [P, MT, 2])
        self.rs4e = sb("rs4e", [P, MT])
        self.rs4 = sb("rs4", [P, MT])
        self.sg = sb("sg", [P, MT, NU])
        self.score = sb("score", [P, MT, NU])
        self.sel = sb("sel", [P, MT, NE])
        self.top = sb("top", [P, MT])
        self.eq = sb("eq", [P, MT, NE])
        self.rank = sb("rank", [P, MT, NE])
        self.first = sb("first", [P, MT])
        self.onehot = sb("onehot", [P, MT, NE])
        self.picked = sb("picked", [P, MT, NE])
        self.tops = sb("tops", [P, MT])
        self.diff = sb("diff", [P, MT])
        self.tdiff = sb("tdiff", [P, MT])
        self.ew = sb("ew", [P, MT])
        self.ow = sb("ow", [P, MT, NU])
        self.owT = sb("owT", [NU, NM])
        n = lambda k: sem("d_" + k)
        self.loaded, self.w12_loaded = n("loaded"), [n("w12_loaded_even"), n("w12_loaded_odd")]
        self.g_w3, self.p_mm, self.p_out = n("g_w3"), n("p_mm"), n("p_out")
        self.ix_loaded, self.ix, self.keep, self.scatter = n("index_loaded"), n("index"), n("keep"), n("scatter")
        self.gather = n("gather")
        self.xgT_mm, self.xgT_out, self.lg_mm, self.lg_sig = n("xgT_mm"), n("xgT_out"), n("lg_mm"), n("lg_sig")
        self.gate, self.sig2, self.owT_mm, self.owT_out, self.c_mm = n("gate"), n("sig2"), n("owT_mm"), n("owT_out"), n("c_mm")
        self.lg_sum, self.c_sum = n("lg_sum"), n("c_sum")
        self.h_mm, self.h_act, self.z1_s, self.z_s, self.zT_mm = n("h_mm"), n("h_act"), n("z1"), n("z"), n("zT_mm")
        self.st_s, self.mv_s, self.rs_s, self.al_s, self.o_mm, self.acc_s = n("st"), n("mv"), n("rs"), n("alpha"), n("o_mm"), n("acc")
        self.st4_s, self.mv4_s, self.rs4_s, self.yo_s = n("st4"), n("mv4"), n("rs4"), n("yo")
        self.rs4e_s = n("rs4e")

    LOADS = 9
    gather_ready, same_ready, scatter_ready = 14, 14 + MT, 14 + 2 * MT + 2
    diff_ready, gate_ready = 10, 13

    def units(self, eng, unit):
        unit(0, 0)
        unit(1, 1)
        with eng.Fori(1, NU // 2) as i:
            for k in range(2):
                unit(i * 2 + k, k)
        unit(NU - 1, 0)

    def index_loads(self, sp):
        sp.dma_start(self.idx[:, :, 0:MT], self.g["idx_cols"]).then_inc(self.ix_loaded, 16)
        sp.dma_start(self.idx[:, :, MT:], self.g["idx_rows"].to_broadcast([P, 2, NM])).then_inc(self.ix_loaded, 16)

    def loads(self, sp):
        g = self.g
        for dst, src in ((self.w3[:], g["w3_units"]), (self.b1[:], g["b1_units"]), (self.b2[:], g["b2_units"]),
                         (self.lng[:], g["lng_units"]), (self.lnb[:], g["lnb_units"]), (self.b3[:], g["b3_units"]),
                         (self.gate_w[:], g["gate_w"]), (self.gate_b[:], g["gate_b"].to_broadcast([P, NU])),
                         (self.exp_bias[:], g["exp_bias"].to_broadcast([P, NE]))):
            sp.dma_start(dst, src).then_inc(self.loaded, 16)
        for n in range(2):
            sp.dma_start(self.w12[n][:], g["w12_units"][n]).then_inc(self.w12_loaded[n], 16)

    def more_loads(self, sp):
        def load(n, k):
            if not isinstance(n, int) or n >= 2:
                after(sp, self.h_mm, 1, n - 2, 1)
                sp.dma_start(self.w12[k][:], self.g["w12_units"][n]).then_inc(self.w12_loaded[k], 16)
        self.units(sp, load)

    def prep_gpsimd(self, pool):
        gp = self.nc.gpsimd
        pool.wait_ge(self.loaded, 16 * self.LOADS)
        gp.memset(self.lnb_diag[:], 0.0).then_inc(self.g_w3, 1)
        gp.tensor_tensor(self.w3g[:], self.w3[:], self.lng[:].unsqueeze(2).to_broadcast([P, NU, D]), ALU.mult).then_inc(self.g_w3, 1)
        gp.tensor_scalar(self.hb1[:], self.b1[:], 0.5, 1.0, ALU.mult, ALU.mult).then_inc(self.g_w3, 1)
        pool.wait_ge(self.g_w3, 1)
        gp.tensor_copy(self.lnb_diag[:].rearrange("p a b -> p (a b)")[:, 0:NU * NU:NU + 1], self.lnb[:]).then_inc(self.g_w3, 1)

    def prep_rows(self, pool):
        for j in range(MT):
            pool.wait_ge(self.ix, self.same_ready - MT + j + 1)
            self.nc.gpsimd.affine_select(out=self.same[j], in_=self.same[j], compare_op=ALU.is_gt, fill=0.0,
                                         base=j * P, pattern=[[-1, NM]], channel_multiplier=1).then_inc(self.keep, 1)

    def prep_bank(self, k):
        return (self.PX[:, 0:512], self.PX[:, 512:1024], self.PA[:])[k % 3]

    PREP = (NU + 1) // 2
    def prep_tensor(self, pe, k):
        mm = self.nc.tensor.matmul
        if k == 0:
            pe.wait_ge(self.g_w3, 4)
            pe.wait_ge(self.ft_out, 2 * B)
        if k == 2:
            pe.wait_ge(self.y1_sum, B)
        if 3 <= k <= self.PREP:
            pe.wait_ge(self.p_out, k - 2)
        if k < self.PREP:
            for j, n in enumerate(range(2 * k, min(2 * k + 2, NU))):
                last = mm(self.prep_bank(k)[:, j * D:(j + 1) * D], self.cst[:, C_CTR:C_CTR + P], self.w3g[:, n, :], start=True, stop=True)
            last.then_inc(self.p_mm, 1)
            return
        o, part = self.PA[0:NU, 0:D], NU // 3
        for n in range(part * (k - self.PREP), part * (k - self.PREP + 1)):
            mm(o, self.lnb_diag[:, n, :], self.w3[:, n, :], start=n == 0, stop=False)
        if k == self.PREP + 2:
            mm(o, self.ident[0:NU, 0:NU], self.b3[:], start=False, stop=True).then_inc(self.p_mm, 1)

    def prep_scalar(self, act, k):
        act.wait_ge(self.p_mm, k + 1)
        if k < self.PREP:
            u = min(2, NU - 2 * k)
            self.nc.scalar.activation(self.w3c[:, 2 * k:2 * k + u, :].rearrange("p u d -> p (u d)"),
                                      self.prep_bank(k)[:, 0:u * D], ACT.Copy).then_inc(self.p_out, 1)
        else:
            self.nc.scalar.activation(self.c3[:], self.PA[0:NU, 0:D], ACT.Copy).then_inc(self.p_out, 1)

    def index_link(self, dve, ins, event):
        ins.then_inc(self.ix, 1)
        dve.wait_ge(self.ix, event)

    def prep_numbers(self, dve):
        v, link, k = self.nc.vector, self.index_link, 1
        dve.wait_ge(self.ix_loaded, 32)
        link(dve, v.tensor_copy(self.idx_f, self.idx[:]), k)
        for axis, size in enumerate((B, T)):
            f, w = self.idx_f[:, axis, :], self.idx_w[:, axis, :]
            link(dve, v.tensor_scalar(w, f, 0.0, float(size), ALU.is_lt, ALU.mult), k + 1)
            link(dve, v.tensor_tensor(w, f, w, ALU.add), k + 2)
            link(dve, v.tensor_scalar(f, w, 0.0, float(size - 1), ALU.max, ALU.min), k + 3)
            link(dve, v.tensor_tensor(w, f, w, ALU.is_equal), k + 4)
            k += 4
        number, inside = self.idx_f[:, 0, :], self.idx_w[:, 0, :]
        link(dve, v.scalar_tensor_tensor(out=number, in0=number, scalar=float(T), in1=self.idx_f[:, 1, :],
                                         op0=ALU.mult, op1=ALU.add), k + 1)
        link(dve, v.tensor_tensor(inside, inside, self.idx_w[:, 1, :], ALU.mult), k + 2)
        link(dve, v.tensor_scalar(inside, inside, -FAR, FAR, ALU.mult, ALU.add), k + 3)
        link(dve, v.tensor_tensor(self.row_to[:], number, inside, ALU.add), k + 4)
        link(dve, v.tensor_copy(self.src_row[:], number[:, 0:MT]), k + 5)
        assert k + 5 == self.gather_ready

    def prep_same(self, dve):
        for j in range(MT):
            self.nc.vector.tensor_scalar(self.same[j], self.row_to[:, MT:], self.row_to[:, j:j + 1], 1.0,
                                         ALU.is_equal, ALU.mult).then_inc(self.ix, 1)

    def prep_targets(self, dve):
        v, k = self.nc.vector, self.same_ready
        for j in range(MT):
            dve.wait_ge(self.keep, j + 1)
            v.tensor_reduce(self.dup[:, j:j + 1], self.same[j], AX_X, ALU.max).then_inc(self.ix, 1)
        dve.wait_ge(self.ix, k + MT)
        self.index_link(dve, v.scalar_tensor_tensor(out=self.to_f[:], in0=self.dup[:], scalar=FAR, in1=self.row_to[:, 0:MT],
                                                    op0=ALU.mult, op1=ALU.add), k + MT + 1)
        v.tensor_copy(self.dst_row[:], self.to_f[:]).then_inc(self.ix, 1)

    def gather_rows(self, pool):
        gp = self.nc.gpsimd
        pool.wait_ge(self.x2_stored, 16 * B)
        pool.wait_ge(self.ix, self.gather_ready)
        for j in range(MT):
            gp.indirect_dma_start(out=self.xg[:, j, :], out_offset=None, in_=self.x2_dram,
                                  in_offset=bass.IndirectOffsetOnAxis(ap=self.src_row[:, j:j + 1], axis=0),
                                  bounds_check=B * T - 1, oob_is_err=False).then_inc(self.gather, 16)

    def gpsimd(self, pool):
        gp = self.nc.gpsimd
        pool.wait_ge(self.gate, self.gate_ready)

        def unit(n, k):
            after_plainly(pool, self.zeroed, (self.mv_s, MT, n, MT), (self.al_s, 1, n - 1, 1))
            gp.tensor_scalar(self.rs[:], self.mv[:, :, 1], 4 * EPS_LN, 1.0, ALU.add, ALU.mult).then_inc(self.rs_s, 1)
            after(pool, self.rs_s, 2, n, 1)
            gp.tensor_tensor(self.rs[:], self.rs[:], self.minus_half[:], ALU.pow).then_inc(self.rs_s, 1)
            after(pool, self.rs_s, 2, n, 2)
            after(pool, self.acc_s, MT, n - 2, MT)
            gp.tensor_tensor(self.alpha[k][:], self.rs[:], self.ow[:, :, n:n + 1].rearrange("p t n -> p (t n)")
                             if isinstance(n, int) else self.ow[:, :, bass.ds(n, 1)].rearrange("p t n -> p (t n)"),
                             ALU.mult).then_inc(self.al_s, 1)

        self.units(pool, unit)
        for half in range(2):
            some = slice(2 * half, 2 * half + 2)
            pool.wait_ge(self.mv4_s, 2 * half + 2)
            gp.tensor_scalar(self.rs4e[:, some], self.mv4[:, some, 1], EPS_LN, 1.0, ALU.add, ALU.mult).then_inc(self.rs4e_s, 1)
            pool.wait_ge(self.rs4e_s, half + 1)
            gp.tensor_tensor(self.rs4[:, some], self.rs4e[:, some], self.minus_half[:, some], ALU.pow).then_inc(self.rs4_s, 1)
        pool.wait_ge(self.out_stored, 16 * B)
        pool.wait_ge(self.ix, self.scatter_ready)
        rows_out = self.out.rearrange("b t d -> (b t) d")
        for j in range(MT):
            pool.wait_ge(self.yo_s, j + 1)
            gp.indirect_dma_start(out=rows_out, out_offset=bass.IndirectOffsetOnAxis(ap=self.dst_row[:, j:j + 1], axis=0),
                                  in_=self.yo[:, j, :], in_offset=None,
                                  bounds_check=B * T - 1, oob_is_err=False).then_inc(self.scatter, 16)
        pool.wait_ge(self.scatter, 16 * MT)

    def out_bank(self, t):
        return (self.PA, self.PB)[t // 2][:, (t % 2) * D:(t % 2 + 1) * D]

    def tensor(self, pe):
        mm, tr = self.nc.tensor.matmul, self.nc.tensor.transpose
        H_ = (self.PX, self.PS)
        pe.wait_ge(self.gather, 16 * MT)
        pe.wait_ge(self.p_out, self.PREP + 1)
        for c in range(DC):
            for t in range(MT):
                last = tr(self.PX[:, c * NM + t * P:c * NM + (t + 1) * P], self.xg[:, t, c * P:(c + 1) * P], self.ident)
            last.then_inc(self.xgT_mm, 1)
        pe.wait_ge(self.xgT_out, 2)

        def hidden(n, k):
            pe.wait_ge(self.w12_loaded[k], (n - k) * 8 + 16)
            after(pe, self.h_act, 2, n - 2, 2)
            after(pe, self.z1_s, 1, n - 2, 1)
            for r in range(2):
                for c in range(DC):
                    last = mm(H_[k][:, r * NM:(r + 1) * NM], self.w12[k][:, r, c, :], self.xgT[:, c, :], start=c == 0, stop=c == DC - 1)
            last.then_inc(self.h_mm, 1)

        def constant_rows():
            pe.wait_ge(self.owT_out, 1)
            after(pe, self.h_act, 2, NU - 2, 2)
            after(pe, self.z1_s, 1, NU - 2, 1)
            for t in range(MT):
                last = mm(self.PS[:, t * D:(t + 1) * D], self.owT[:, t * P:(t + 1) * P], self.c3[:], start=True, stop=True)
            last.then_inc(self.c_mm, 1)

        def unit(n, k):
            if isinstance(n, int) and n == NU - 1:
                constant_rows()
            else:
                hidden(n + 1, 1 - k)
            after(pe, self.z_s, 1, n, 1)
            after(pe, self.st_s, MT, n - 1, MT)
            for t in range(MT):
                last = tr(self.PT[:, t * P:(t + 1) * P], self.z[k][:, t * P:(t + 1) * P], self.ident)
            last.then_inc(self.zT_mm, 1)
            after(pe, self.acc_s, MT, n - 1, MT)
            w = self.w3c[:, n, :] if isinstance(n, int) else self.w3c[:, bass.ds(n, 1), :].rearrange("p n d -> p (n d)")
            for t in range(MT):
                last = mm(self.out_bank(t), self.z[k][:, t * P:(t + 1) * P], w, start=True, stop=True)
                if t % 2 == 1:
                    last.then_inc(self.o_mm, 1)
            if isinstance(n, int) and n == 1:
                pe.wait_ge(self.gate, self.gate_ready)
                for t in range(MT):
                    last = tr(self.PC[0:NU, t * P:(t + 1) * P], self.ow[:, t, :], self.ident)
                last.then_inc(self.owT_mm, 1)

        hidden(0, 0)
        pe.wait_ge(self.y3_sum, B * TT)
        for t in range(MT):
            o = self.PC[:, t * NU:(t + 1) * NU]
            for c in range(DC):
                last = mm(o, self.xgT[:, c, t * P:(t + 1) * P], self.gate_w[:, c, :], start=c == 0, stop=c == DC - 1)
        last.then_inc(self.lg_mm, 1)
        self.units(pe, unit)

    def scalar(self, act):
        a = self.nc.scalar.activation
        H_ = (self.PX, self.PS)
        for c in range(DC):
            act.wait_ge(self.xgT_mm, c + 1)
            a(self.xgT[:, c, :], self.PX[:, c * NM:(c + 1) * NM], ACT.Copy).then_inc(self.xgT_out, 1)

        def unit(n, k):
            col = lambda b: b[:, n:n + 1] if isinstance(n, int) else b[:, bass.ds(n, 1)]
            after(act, self.h_mm, 1, n, 1)
            after(act, self.z_s, 1, n - 2, 1)
            a(self.th[k][:], H_[k][:, 0:NM], ACT.Tanh, bias=col(self.hb1), scale=0.5).then_inc(self.h_act, 1)
            a(self.h2[k][:], H_[k][:, NM:2 * NM], ACT.Identity, bias=col(self.b2)).then_inc(self.h_act, 1)
            if isinstance(n, int) and n == 0:
                act.wait_ge(self.lg_sum, 1)
                a(self.sg[:], self.sg[:], ACT.Tanh, scale=0.5).then_inc(self.lg_sig, 1)
                act.wait_ge(self.gate, self.diff_ready)
                a(self.tdiff[:], self.diff[:], ACT.Tanh, scale=0.5).then_inc(self.sig2, 1)
            if isinstance(n, int) and n == 1:
                act.wait_ge(self.owT_mm, 1)
                a(self.owT[:], self.PC[0:NU, 0:NM], ACT.Copy).then_inc(self.owT_out, 1)

        self.units(act, unit)

    def vector(self, dve):
        v = self.nc.vector
        H_ = (self.PX, self.PS)
        done = 0

        def link(ins):
            nonlocal done
            done += 1
            ins.then_inc(self.gate, 1)
            dve.wait_ge(self.gate, done)

        def product(n, k):
            b1 = self.b1[:, n:n + 1] if isinstance(n, int) else self.b1[:, bass.ds(n, 1)]
            after(dve, self.h_act, 2, n, 2)
            after(dve, self.z_s, 1, n - 2, 1)
            v.scalar_tensor_tensor(out=self.z1[k][:], in0=H_[k][:, 0:NM], scalar=b1, in1=self.h2[k][:],
                                   op0=ALU.add, op1=ALU.mult).then_inc(self.z1_s, 1)
            after(dve, self.z1_s, 1, n, 1)
            after(dve, self.o_mm, 2, n - 2, 2)
            v.scalar_tensor_tensor(out=self.z[k][:], in0=self.th[k][:], scalar=1.0, in1=self.z1[k][:],
                                   op0=ALU.add, op1=ALU.mult).then_inc(self.z_s, 1)

        wide = lambda ap: ap[:].unsqueeze(2).to_broadcast([P, MT, NE])
        per_tile = lambda ap: ap.unsqueeze(1).to_broadcast([P, MT, NE])
        dve.wait_ge(self.lg_mm, 1)
        v.tensor_tensor(self.sg[:], self.PC[:, 0:MT * NU].rearrange("p (t n) -> p t n", n=NU),
                        self.gate_b[:].unsqueeze(1).to_broadcast([P, MT, NU]), ALU.add).then_inc(self.lg_sum, 1)
        product(0, 0)
        dve.wait_ge(self.lg_sig, 1)
        link(v.tensor_scalar(self.score[:], self.sg[:], 0.5, 0.5, ALU.mult, ALU.add))
        link(v.tensor_tensor(self.sel[:], self.score[:, :, 1:NU], per_tile(self.exp_bias[:]), ALU.add))
        link(v.tensor_reduce(self.top[:], self.sel[:], AX_X, ALU.max))
        link(v.tensor_tensor(self.eq[:], self.sel[:], wide(self.top), ALU.is_equal))
        link(v.tensor_tensor(self.rank[:], self.eq[:], per_tile(self.cst[:, C_REV:C_REV + NE]), ALU.mult))
        link(v.tensor_reduce(self.first[:], self.rank[:], AX_X, ALU.max))
        link(v.tensor_tensor(self.onehot[:], per_tile(self.cst[:, C_REV:C_REV + NE]), wide(self.first), ALU.is_equal))
        link(v.tensor_tensor(self.picked[:], self.onehot[:], self.score[:, :, 1:NU], ALU.mult))
        link(v.tensor_reduce(self.tops[:], self.picked[:], AX_X, ALU.add))
        link(v.tensor_tensor(self.diff[:], self.score[:, :, 0], self.tops[:], ALU.subtract))
        assert done == self.diff_ready
        dve.wait_ge(self.sig2, 1)
        link(v.tensor_scalar(self.ow[:, :, 0], self.tdiff[:], 0.5, 0.5, ALU.mult, ALU.add))
        link(v.tensor_scalar(self.ew[:], self.tdiff[:], -0.5, 0.5, ALU.mult, ALU.add))
        link(v.tensor_tensor(self.ow[:, :, 1:NU], self.onehot[:], wide(self.ew), ALU.mult))
        assert done == self.gate_ready

        def unit(n, k):
            after(dve, self.zT_mm, 1, n, 1)
            after(dve, self.mv_s, MT, n - 1, MT)
            after(dve, self.rs_s, 2, n - 1, 2)
            for t in range(MT):
                v.bn_stats(self.st[:, t, :], self.PT[:, t * P:(t + 1) * P]).then_inc(self.st_s, 1)
            for t in range(MT):
                after_plainly(dve, self.zeroed, (self.st_s, MT, n, t + 1))
                v.bn_aggr(self.mv[:, t, :], self.st[:, t, :]).then_inc(self.mv_s, 1)
            if not (isinstance(n, int) and n == NU - 1):
                product(n + 1, 1 - k)
            first, last = isinstance(n, int) and n == 0, isinstance(n, int) and n == NU - 1
            if last:
                dve.wait_ge(self.c_mm, 1)
                after(dve, self.acc_s, MT, n - 1, MT)
                for half in range(2):
                    some = self.acc[:, 2 * half:2 * half + 2, :].rearrange("p t d -> p (t d)")
                    v.tensor_tensor(some, self.PS[:, 2 * half * D:(2 * half + 2) * D], some, ALU.add).then_inc(self.c_sum, 1)
            into = self.xg if first else self.acc
            after(dve, self.al_s, 1, n, 1)
            for t in range(MT):
                after(dve, self.o_mm, 2, n, t // 2 + 1)
                after(dve, self.acc_s, MT, n - 1, t + 1)
                if last:
                    dve.wait_ge(self.c_sum, t // 2 + 1)
                v.scalar_tensor_tensor(out=self.acc[:, t, :], in0=self.out_bank(t), scalar=self.alpha[k][:, t:t + 1],
                                       in1=into[:, t, :], op0=ALU.mult, op1=ALU.add).then_inc(self.acc_s, 1)
                if last and t % 2 == 1:
                    for u in range(t - 1, t + 1):
                        after(dve, self.acc_s, MT, n, u + 1)
                        v.bn_stats(self.st4[:, u, :], self.acc[:, u, :]).then_inc(self.st4_s, 1)
                    for u in range(t - 1, t + 1):
                        dve.wait_ge(self.st4_s, u + 1)
                        v.bn_aggr(self.mv4[:, u, :], self.st4[:, u, :]).then_inc(self.mv4_s, 1)

        self.units(dve, unit)
        for t in range(MT):
            dve.wait_ge(self.rs4_s, t // 2 + 1)
            v.tensor_scalar(self.yo[:, t, :], self.acc[:, t, :], self.mv4[:, t, 0:1], self.rs4[:, t:t + 1],
                            ALU.subtract, ALU.mult).then_inc(self.yo_s, 1)


def constants():
    f = np.float32
    c = np.zeros((P, C_END), f)
    c[:, C_ID:C_ID + P] = np.eye(P)
    c[:, C_CTR:C_CTR + P] = np.eye(P) - 1.0 / FH
    inv = (1.0 / f(10000.0) ** (np.arange(0, DK, 2, dtype=f) / f(DK))).astype(f)

    def angles(n):
        t = (f(10.0) * (np.arange(n, dtype=f) / f(n))).astype(f)
        return np.outer(t, inv).astype(f)

    aq, ak = angles(T), angles(LK)
    cq = np.concatenate([np.cos(aq), np.cos(aq)], 1)
    sq = np.concatenate([-np.sin(aq), np.sin(aq)], 1)
    for t in range(TT):
        c[:, C_COSQ + t * D:C_COSQ + (t + 1) * D] = np.tile(cq[t * P:(t + 1) * P], (1, H))
        c[:, C_SINQ + t * D:C_SINQ + (t + 1) * D] = np.tile(sq[t * P:(t + 1) * P], (1, H))
    c[:, C_COST:C_COST + T] = np.tile(cq.T, (HC, 1))
    c[:, C_SINT:C_SINT + T] = np.tile(sq.T, (HC, 1))
    c[:, C_COSK:C_COSK + LK] = np.tile(np.concatenate([np.cos(ak), np.cos(ak)], 1).T, (HC, 1))
    c[:, C_SINK:C_SINK + LK] = np.tile(np.concatenate([-np.sin(ak), np.sin(ak)], 1).T, (HC, 1))
    p = np.arange(P)
    for j in range(4):
        c[:, C_MASK + j] = (p // DK) % 4 == j
    for j in range(HC):
        c[:, C_BLOCK + j] = p // DK == j
        c[:, C_HALF + j] = 0.5 * (p // DK == j)
    c[:, C_REV:C_REV + NE] = NE - np.arange(NE)
    return c


def kernel(**inputs):
    import concourse.bacc as bacc
    from concourse.bass_utils import run_bass_kernel_spmd

    i = {k: np.asarray(v) for k, v in inputs.items()}
    a = lambda n: i["L0_attn_" + n]
    x = lambda n: i["L0_xattn_" + n]
    f = lambda n: i["L0_ffn_" + n]
    rot = np.arange(D).reshape(H, 2, DK // 2)[:, ::-1].reshape(-1)

    def by_chunk(m):
        return np.ascontiguousarray(m.reshape(DC, P, -1).transpose(1, 0, 2))

    def vec(v):
        return v.reshape(DC, P).T

    def units(shared, experts):
        return np.concatenate([shared[None], experts])

    arrays = {
        "x": i["x"],
        "xT": np.ascontiguousarray(i["x"].transpose(0, 2, 1).reshape(B, DC, P, T).transpose(0, 2, 1, 3)),
        "ctxT": by_chunk(i["ctx_1024"].transpose(2, 0, 1).reshape(D, CT)),
        "w_aq": by_chunk(a("Wq").T), "w_ak": by_chunk(a("Wk").T), "w_av": by_chunk(a("Wv").T), "w_ao": by_chunk(a("Wo").T),
        "w_xq": by_chunk(x("Wq").T), "w_xk": by_chunk(x("Wk").T), "w_xkr": by_chunk(x("Wk")[rot].T),
        "w_xv": by_chunk(x("Wv").T), "w_xo": by_chunk(x("Wo").T),
        "w_s12": by_chunk(np.concatenate([f("sw1"), f("sw2")]).T), "w3s": np.ascontiguousarray(f("sw3").T),
        "proj": np.ascontiguousarray(a("proj").reshape(DC, HC, M, DK).transpose(1, 3, 0, 2)).reshape(P, DC, M),
        "bo_a": a("bo").reshape(1, D),
        "rows": np.concatenate([x("bo"), f("sb3"), f("sb3")]).reshape(1, 3, D),
        "cols": np.ascontiguousarray(np.concatenate(
            [vec(x("bq")), vec(x("bq")[rot]), vec(x("bk")), vec(x("bk")[rot]), vec(x("bv")),
             f("sb1")[:, None], f("sb2")[:, None], f("s_ln_g")[:, None], f("s_ln_b")[:, None],
             ], 1)),
        "cst": constants(),
        "w12_units": np.ascontiguousarray(units(np.stack([f("sw1"), f("sw2")]), np.stack([f("ew1"), f("ew2")], 1))
                                          .reshape(NU, 2, FH, DC, P).transpose(0, 4, 1, 3, 2)),
        "w3_units": np.ascontiguousarray(units(f("sw3"), f("ew3")).transpose(2, 0, 1)),
        "b1_units": units(f("sb1"), f("eb1")).T.copy(), "b2_units": units(f("sb2"), f("eb2")).T.copy(),
        "lng_units": units(f("s_ln_g"), np.tile(f("sel_ln_g"), (NE, 1))).T.copy(),
        "lnb_units": units(f("s_ln_b"), np.tile(f("sel_ln_b"), (NE, 1))).T.copy(),
        "b3_units": units(f("sb3"), f("eb3")),
        "gate_w": by_chunk(np.concatenate([f("sg_w"), f("eg_w")]).T),
        "gate_b": np.concatenate([f("sg_b"), f("eg_b")]).reshape(1, NU),
        "exp_bias": f("exp_bias").reshape(1, NE),
        "idx_cols": np.ascontiguousarray(np.stack([f("index_b").reshape(MT, P).T, f("index_t").reshape(MT, P).T], 1)),
        "idx_rows": np.stack([f("index_b"), f("index_t")])[None],
    }
    nc = bacc.Bacc("TRN2", target_bir_lowering=False, num_devices=1)
    g = {n: nc.dram_tensor("in_" + n, v.shape, mybir.dt.from_np(v.dtype), kind="ExternalInput").ap() for n, v in arrays.items()}
    out = nc.dram_tensor("out_0", (B, T, D), F32, kind="ExternalOutput").ap()
    decoder_layer(nc, g, out)
    r = run_bass_kernel_spmd(nc, [{"in_" + n: v for n, v in arrays.items()}], core_ids=[0])
    return r.results[0]["out_0"]
```
